# Optimizing a Trainium2 kernel written in Bass

```python
import numpy as np
import jax
import jax.numpy as jnp

def _softmax(x, axis=-1):
    return jax.nn.softmax(x, axis=axis)

def _gelu(x):
    return jax.nn.gelu(x, approximate=True)

def _silu(x):
    return jax.nn.silu(x)

def _sigmoid(x):
    return jax.nn.sigmoid(x)

def _layernorm(x, axis=-1, eps=1e-05):
    m = jnp.mean(x, axis=axis, keepdims=True)
    v = jnp.var(x, axis=axis, keepdims=True)
    return (x - m) / jnp.sqrt(v + eps)

def _scatter_add(tgt, idx, src, axis=0):
    return tgt.at[idx].add(src)

def _segment_sum(src, seg, n):
    return jax.ops.segment_sum(src, seg, n)
kernel_name = 'mk_prb_d1_jaxref_r8_8f213f'

def setup_inputs(seed: int=0):
    np.random.seed(seed)
    _w = jnp.asarray

    def _L0_attn_setup():
        import jax, jax.numpy as jnp
        import numpy as np
        B, T, C, R = (8, 128, 128, 64)
        EPS = 1e-05
        key = jax.random.key(seed)
        ks = jax.random.split(key, 8)
        x = jax.random.normal(ks[0], (B, T, C), dtype=jnp.float32)
        W_attn = jax.random.normal(ks[1], (3 * C, C), dtype=jnp.float32) * 0.02
        W_proj = jax.random.normal(ks[2], (C, C), dtype=jnp.float32) * 0.02
        lora_attn_A = jax.random.normal(ks[3], (C, R), dtype=jnp.float32) * 0.02
        lora_attn_B = jax.random.normal(ks[4], (R, 3 * C), dtype=jnp.float32) * 0.02
        lora_proj_A = jax.random.normal(ks[5], (C, R), dtype=jnp.float32) * 0.02
        lora_proj_B = jax.random.normal(ks[6], (R, C), dtype=jnp.float32) * 0.02
        bn_gamma = jnp.ones((3 * C,), dtype=jnp.float32)
        bn_beta = jnp.zeros((3 * C,), dtype=jnp.float32)
        return {'x': x, 'W_attn': W_attn, 'W_proj': W_proj, 'lora_attn_A': lora_attn_A, 'lora_attn_B': lora_attn_B, 'lora_proj_A': lora_proj_A, 'lora_proj_B': lora_proj_B, 'bn_gamma': bn_gamma, 'bn_beta': bn_beta}
    _L0_attn_in = _L0_attn_setup()

    def _L0_ffn_setup():
        import jax, jax.numpy as jnp
        import numpy as np
        EPS = 1e-06
        LN_EPS = 1e-05

        def _absmean_core(W):
            gamma = jnp.mean(jnp.abs(W)) + EPS
            Ws = W / gamma
            Wq = jnp.sign(Ws) * jnp.minimum(jnp.round(jnp.abs(Ws)), 1.0)
            return (Wq, gamma)

        @jax.custom_vjp
        def absmean(W):
            return _absmean_core(W)[0]

        def _absmean_fwd(W):
            Wq, gamma = _absmean_core(W)
            return (Wq, gamma)

        def _absmean_bwd(gamma, g):
            return (g / gamma,)
        absmean.defvjp(_absmean_fwd, _absmean_bwd)

        def layernorm(x, w, b, eps=LN_EPS):
            mu = jnp.mean(x, axis=-1, keepdims=True)
            var = jnp.mean((x - mu) ** 2, axis=-1, keepdims=True)
            return (x - mu) * jax.lax.rsqrt(var + eps) * w + b
        key = jax.random.key(seed)
        k1, k2, k3 = jax.random.split(key, 3)
        d, h = (128, 512)
        B, T = (8, 256)
        return {'x': jax.random.normal(k1, (B, T, d), jnp.float32), 'W_fc': jax.random.normal(k2, (h, d), jnp.float32), 'ln_w': jnp.ones((h,), jnp.float32), 'ln_b': jnp.zeros((h,), jnp.float32), 'W_proj': jax.random.normal(k3, (d, h), jnp.float32)}
    _L0_ffn_in = _L0_ffn_setup()
    _d = {'L0_attn_x': _L0_attn_in['x'], 'L0_attn_W_attn': _L0_attn_in['W_attn'], 'L0_attn_W_proj': _L0_attn_in['W_proj'], 'L0_attn_lora_attn_A': _L0_attn_in['lora_attn_A'], 'L0_attn_lora_attn_B': _L0_attn_in['lora_attn_B'], 'L0_attn_lora_proj_A': _L0_attn_in['lora_proj_A'], 'L0_attn_lora_proj_B': _L0_attn_in['lora_proj_B'], 'L0_attn_bn_gamma': _L0_attn_in['bn_gamma'], 'L0_attn_bn_beta': _L0_attn_in['bn_beta'], 'L0_ffn_W_fc': _L0_ffn_in['W_fc'], 'L0_ffn_ln_w': _L0_ffn_in['ln_w'], 'L0_ffn_ln_b': _L0_ffn_in['ln_b'], 'L0_ffn_W_proj': _L0_ffn_in['W_proj']}
    _x0 = _d['L0_attn_x']
    _d['L0_attn_x'] = jax.random.normal(jax.random.fold_in(jax.random.key(seed), 1), (4, 1024, 128), dtype=_x0.dtype)
    del _x0
    return _d

def reference(L0_attn_x, L0_attn_W_attn, L0_attn_W_proj, L0_attn_lora_attn_A, L0_attn_lora_attn_B, L0_attn_lora_proj_A, L0_attn_lora_proj_B, L0_attn_bn_gamma, L0_attn_bn_beta, L0_ffn_W_fc, L0_ffn_ln_w, L0_ffn_ln_b, L0_ffn_W_proj):

    def _L0_attn_ref(x, W_attn, W_proj, lora_attn_A, lora_attn_B, lora_proj_A, lora_proj_B, bn_gamma, bn_beta):
        import jax, jax.numpy as jnp
        import numpy as np
        B, T, C, R = (8, 128, 128, 64)
        EPS = 1e-05
        Bb, Tt, Cc = x.shape
        Wm_attn = W_attn + (lora_attn_A @ lora_attn_B).reshape(W_attn.shape)
        xa = jnp.einsum('btc,dc->btd', x, Wm_attn)
        mean = xa.mean(axis=(0, 1))
        var = xa.var(axis=(0, 1))
        xa = (xa - mean) * jax.lax.rsqrt(var + EPS) * bn_gamma + bn_beta
        q, k, v = jnp.split(xa, 3, axis=-1)
        scale = 1.0 / jnp.sqrt(jnp.asarray(Cc, dtype=x.dtype))
        att = jnp.einsum('btc,bsc->bts', q, k) * scale
        causal = jnp.tril(jnp.ones((Tt, Tt), dtype=bool))
        att = jnp.where(causal[None, :, :], att, -jnp.inf)
        att = jax.nn.softmax(att, axis=-1)
        y = jnp.einsum('bts,bsc->btc', att, v)
        y = jnp.einsum('btc,dc->btd', y, W_proj)
        Wm_proj = W_proj + (lora_proj_A @ lora_proj_B).reshape(W_proj.shape)
        y = jnp.einsum('btc,dc->btd', y, Wm_proj)
        return y

    def _L0_ffn_ref(x, W_fc, ln_w, ln_b, W_proj):
        import jax, jax.numpy as jnp
        import numpy as np
        EPS = 1e-06
        LN_EPS = 1e-05

        def _absmean_core(W):
            gamma = jnp.mean(jnp.abs(W)) + EPS
            Ws = W / gamma
            Wq = jnp.sign(Ws) * jnp.minimum(jnp.round(jnp.abs(Ws)), 1.0)
            return (Wq, gamma)

        @jax.custom_vjp
        def absmean(W):
            return _absmean_core(W)[0]

        def _absmean_fwd(W):
            Wq, gamma = _absmean_core(W)
            return (Wq, gamma)

        def _absmean_bwd(gamma, g):
            return (g / gamma,)
        absmean.defvjp(_absmean_fwd, _absmean_bwd)

        def layernorm(x, w, b, eps=LN_EPS):
            mu = jnp.mean(x, axis=-1, keepdims=True)
            var = jnp.mean((x - mu) ** 2, axis=-1, keepdims=True)
            return (x - mu) * jax.lax.rsqrt(var + eps) * w + b
        h = jnp.einsum('btd,hd->bth', x, absmean(W_fc))
        h = jax.nn.gelu(h, approximate=False)
        h = layernorm(h, ln_w, ln_b)
        return jnp.einsum('bth,dh->btd', h, absmean(W_proj))
    x = L0_attn_x
    xn = _layernorm(x, axis=-1)
    x = x + _L0_attn_ref(xn, L0_attn_W_attn, L0_attn_W_proj, L0_attn_lora_attn_A, L0_attn_lora_attn_B, L0_attn_lora_proj_A, L0_attn_lora_proj_B, L0_attn_bn_gamma, L0_attn_bn_beta) + _L0_ffn_ref(xn, L0_ffn_W_fc, L0_ffn_ln_w, L0_ffn_ln_b, L0_ffn_W_proj)
    return x

_drawn_inputs = setup_inputs


def setup_inputs(seed=0):
    import zlib

    import numpy as np

    out = dict(_drawn_inputs(seed))
    spreads = {'L0_attn_bn_gamma': (1.0, 0.6),
     'L0_attn_bn_beta': (0.0, 0.8),
     'L0_ffn_ln_w': (1.0, 0.2),
     'L0_ffn_ln_b': (0.0, 0.1)}
    factors = {'L0_attn_W_attn': 8.0,
     'L0_attn_W_proj': 8.0,
     'L0_attn_lora_attn_A': 8.0,
     'L0_attn_lora_attn_B': 8.0,
     'L0_attn_lora_proj_A': 8.0,
     'L0_attn_lora_proj_B': 8.0}
    for name, (base, spread) in spreads.items():
        noise = np.random.default_rng([zlib.crc32(name.encode()), seed]).standard_normal(out[name].shape)
        drawn = base * np.exp(spread * noise) if base else spread * noise
        out[name] = jnp.asarray(drawn.astype(out[name].dtype))
    for name, factor in factors.items():
        out[name] = (out[name] * factor).astype(out[name].dtype)
    return out
```

```python
from contextlib import ExitStack

import concourse.bass as bass
from concourse import mybir

F32, F16, BF16 = mybir.dt.float32, mybir.dt.float16, mybir.dt.bfloat16
ALU = mybir.AluOpType
ACT = mybir.ActivationFunctionType
AXX = mybir.AxisListType.X
REDUCE_ABSMAX = bass.bass_isa.ReduceOp.absmax

P = 128
BATCH, T, C, R, H = 4, 1024, 128, 64, 512
TOKENS = BATCH * T
NT = TOKENS // P
GT = 4
NG = NT // GT
QT = T // P
HC = H // P
LN_EPS, BN_EPS, Q_EPS = 1e-5, 1e-5, 1e-6

XS = 16.0
MS = 16.0
ZS = 64.0
LN_PS = 8.317766166719343
SLOTS = 2
MASKED = -float(2 ** 36)

CHUNKS = [1 if i < GT else 2 for i in range(QT)]
CHUNK0 = [sum(CHUNKS[:i]) for i in range(QT)]
BATCH_CHUNKS = sum(CHUNKS)

W_FC, W_PF, W_QKV, W_QKVT, W_O, W_OT, W_COLS = 0, 512, 1024, 1408, 1792, 1920, 2048
N_COLS = 2 * HC + 6
L_AT, L_B, L_PAT, L_PB, L_END = 0, 128, 512, 640, 768


def block_kernel(nc, x_d, w_d, lora_d, out_d):
    x_v = x_d.rearrange("b (n p) c -> p (b n) c", p=P)
    out_v = out_d.rearrange("b (n p) c -> p (b n) c", p=P)
    with ExitStack() as ctx:
        def sb(name, shape, dt=F32):
            return ctx.enter_context(nc.sbuf_tensor(name, shape, dt))

        def sem(name):
            return ctx.enter_context(nc.semaphore(name))

        x_sb = sb("x_sb", [P, NT, C])
        w_sb = sb("w_sb", [P, W_COLS + N_COLS])
        lora_sb = sb("lora_sb", [R, L_END])
        ident = sb("ident", [P, P])
        ident_bf = sb("ident_bf", [P, P], BF16)
        mask_bf = sb("mask_bf", [P, P], BF16)
        ones = sb("ones", [P, P])
        az = sb("az", [R, 3, 3 * C])
        neg_half = sb("neg_half", [P, 2 * GT])
        xn_ring = sb("xn_ring", [P, 2, GT, C + 1])
        xT_hi = sb("xT_hi", [P, TOKENS], F16)
        xT_lo = sb("xT_lo", [P, TOKENS], F16)
        ln_st = sb("ln_st", [P, NT, 6])
        ln_tmp = sb("ln_tmp", [P, 6, 2 * GT])
        ln_nmean = sb("ln_nmean", [P, NT])
        ln_arg = sb("ln_arg", [P, NT])
        ln_r = sb("ln_r", [P, NT])
        ln_nb = sb("ln_nb", [P, NT])
        wabs = sb("wabs", [P, 2])
        thr = sb("thr", [P, 4])
        below = sb("below", [P, H], F16)
        wq_fc = sb("wq_fc", [P, H], F16)
        wq_pf = sb("wq_pf", [P, HC, C], F16)
        wq_pf32 = sb("wq_pf32", [P, HC, C])
        lnb_bc = sb("lnb_bc", [P, HC, P])
        lnw_abs = sb("lnw_abs", [P, 2])
        lnw_s = sb("lnw_s", [P, HC])
        ffn_scale = sb("ffn_scale", [P, 2])
        wm = sb("wm", [P, 3, C])
        wmT = sb("wmT", [P, 3 * C])
        woT = sb("woT", [P, C])
        two_proj = sb("two_proj", [P, C])
        gram = sb("gram", [P, C + 1])
        bn_prod = sb("bn_prod", [P, C])
        bn = sb("bn", [P, 14, 3])
        wq_scaled = sb("wq_scaled", [P, C])
        wv_scaled = sb("wv_scaled", [P, C])
        bv_bc = sb("bv_bc", [P, P])
        amax = sb("amax", [P, 10])
        m_f = sb("m_f", [P, C + 1])
        u_f = sb("u_f", [P, C])
        m_hi = sb("m_hi", [P, C], F16)
        m_lo = sb("m_lo", [P, C], F16)
        u_hi_w = sb("u_hi_w", [P, C], F16)
        u_lo_w = sb("u_lo_w", [P, C], F16)
        bias4 = sb("bias4", [P, GT, C])
        g_ring = sb("g_ring", [P, 2, GT, H])
        fst = sb("fst", [P, 2, GT, 6])
        f_tmp = sb("f_tmp", [P, 2, 5, GT])
        f_r = sb("f_r", [P, 2, 2, GT])
        z_hi = sb("z_hi", [P, 2, HC, GT * P], F16)
        z_lo = sb("z_lo", [P, 2, HC, GT * P], F16)
        qT_hi = sb("qT_hi", [P, TOKENS], F16)
        qT_lo = sb("qT_lo", [P, TOKENS], F16)
        u_hi = sb("u_hi", [P, NT, C], F16)
        u_lo = sb("u_lo", [P, NT, C], F16)
        e_ring = sb("e_ring", [P, 2, T])
        eT_hi = sb("eT_hi", [P, 2, QT, P], F16)
        eT_lo = sb("eT_lo", [P, 2, QT, P], F16)
        nmax = sb("nmax", [P, 2])
        nbias = sb("nbias", [P, 2])
        rowsum = sb("rowsum", [P, 2])
        rinv = sb("rinv", [P, 2, 2])

        banks = ctx.enter_context(nc.psum_tensor("banks", [P, 8, 512], F32))

        cols = w_sb[:, W_COLS:W_COLS + N_COLS]
        lnw_c, lnb_c = cols[:, 0:HC], cols[:, HC:2 * HC]
        gamma_c, beta_c = cols[:, 2 * HC:2 * HC + 3], cols[:, 2 * HC + 3:2 * HC + 6]

        x_in = [sem(f"x_in{k}") for k in range(4)]
        wfc_in, w_in, lora_in = sem("wfc_in"), sem("w_in"), sem("lora_in")
        consts = sem("consts")
        dve_seq = sem("dve_seq")
        act_seq = sem("act_seq")
        pool_seq = sem("pool_seq")
        wabs_done, thr_sum = sem("wabs_done"), sem("thr_sum")
        wq_fc_done, wq_pf_done = sem("wq_fc_done"), sem("wq_pf_done")
        ln_arg_done, ln_pow, ln_nb_done = sem("ln_arg_done"), sem("ln_pow"), sem("ln_nb_done")
        xn_done, xT_done, xhi_done, xlo_done, gram_done = (
            sem("xn_done"), sem("xT_done"), sem("xhi_done"), sem("xlo_done"), sem("gram_done"))
        prep_mm, prep_wm, woT_done, two_mm, two_done = (
            sem("prep_mm"), sem("prep_wm"), sem("woT_done"), sem("two_mm"), sem("two_done"))
        lnw_red, lnw_all, lnw_done = sem("lnw_red"), sem("lnw_all"), sem("lnw_done")
        h_done, gelu_done, farg_done, z_done = sem("h_done"), sem("gelu_done"), sem("farg_done"), sem("z_done")
        zT_done, zhi_done, zlo_done, f_done, fadd_done = (
            sem("zT_done"), sem("zhi_done"), sem("zlo_done"), sem("f_done"), sem("fadd_done"))
        gram_cp, bn_z, bn_arg, bn_pow, bn_w, m_mm = (
            sem("gram_cp"), sem("bn_z"), sem("bn_arg"), sem("bn_pow"), sem("bn_w"), sem("m_mm"))
        m_abs, m_all, m_split, bias_done = sem("m_abs"), sem("m_all"), sem("m_split"), sem("bias_done")
        q_mm, qhi_done, qlo_done = sem("q_mm"), sem("qhi_done"), sem("qlo_done")
        u_mm, uhi_done, ulo_done, badd_done = sem("u_mm"), sem("uhi_done"), sem("ulo_done"), sem("badd_done")
        s_done, nb_done, exp_done, eT_done, ehi_done, elo_done, pv_done, fin_done = (
            sem("s_done"), sem("nb_done"), sem("exp_done"), sem("eT_done"), sem("ehi_done"),
            sem("elo_done"), sem("pv_done"), sem("fin_done"))
        out_done = sem("out_done")

        block = ctx.enter_context(nc.Block())

        def wait(eng, semaphore, value):
            if not isinstance(value, int) or value > 0:
                eng.wait_ge(semaphore, value)

        class Sequence:

            def __init__(self, eng, semaphore):
                self.eng, self.semaphore, self.count = eng, semaphore, 0

            def mark(self, instruction):
                instruction.then_inc(self.semaphore, 1)
                self.count = self.count + 1

            def settle(self):
                self.eng.wait_ge(self.semaphore, self.count)

            def link(self, instruction):
                self.mark(instruction)
                self.settle()

        def tokens(n, k=1):
            return bass.ds(n * P, k * P)

        @block.sync
        def _(sp):
            sp.dma_start(w_sb[:, W_FC:W_PF], w_d[:, W_FC:W_PF]).then_inc(wfc_in, 16)
            for k in range(4):
                sp.dma_start(x_sb[:, 8 * k:8 * k + 8, :], x_v[:, 8 * k:8 * k + 8, :]).then_inc(x_in[k], 16)
            with sp.Fori(0, NT) as n:
                sp.wait_ge(fin_done, n + 1 + SLOTS)
                sp.dma_start(out_v[:, bass.ds(n, 1), :], x_sb[:, bass.ds(n, 1), :]).then_inc(out_done, 16)
            sp.wait_ge(out_done, 16 * NT)

        @block.gpsimd
        def _(pool):
            seq = Sequence(pool, pool_seq)
            nc.gpsimd.memset(ones[:], 1.0).then_inc(consts, 1)
            seq.mark(nc.gpsimd.memset(neg_half[:], -0.5))
            seq.mark(nc.gpsimd.memset(ident[:], 0.0))
            seq.mark(nc.gpsimd.memset(ident_bf[:], 0.0))
            seq.mark(nc.gpsimd.memset(mask_bf[:], 0.0))
            seq.mark(nc.gpsimd.memset(az[:], 0.0))
            seq.settle()
            nc.gpsimd.affine_select(out=ident[:], in_=ident[:], compare_op=ALU.not_equal, fill=1.0,
                                    base=0, pattern=[[-1, P]], channel_multiplier=1).then_inc(consts, 1)
            nc.gpsimd.memset(xn_ring[:, :, :, C:C + 1], 1.0).then_inc(consts, 1)
            nc.gpsimd.affine_select(out=ident_bf[:], in_=ident_bf[:], compare_op=ALU.not_equal, fill=1.0,
                                    base=0, pattern=[[-1, P]], channel_multiplier=1).then_inc(consts, 1)
            nc.gpsimd.affine_select(out=mask_bf[:], in_=mask_bf[:], compare_op=ALU.is_ge, fill=MASKED,
                                    base=0, pattern=[[-1, P]], channel_multiplier=1).then_inc(consts, 1)
            pool.wait_ge(lora_in, 16)
            for m in range(3):
                spread = az[:, m, :].rearrange("r (i three) -> r i three", three=3)[:, :, m]
                nc.gpsimd.tensor_copy(spread, lora_sb[:, L_AT:L_AT + C]).then_inc(consts, 1)

            def ln_root(p):
                pool.wait_ge(ln_arg_done, p + 1)
                nc.gpsimd.tensor_tensor(ln_r[:, bass.ds(8 * p, 8)], ln_arg[:, bass.ds(8 * p, 8)], neg_half[:],
                                        ALU.pow).then_inc(ln_pow, 1)

            ln_root(0)
            pool.wait_ge(lnw_red, 1)
            nc.gpsimd.partition_all_reduce(lnw_abs[:, 1:2], lnw_abs[:, 0:1], P, REDUCE_ABSMAX).then_inc(lnw_all, 1)
            with pool.Fori(1, 4) as p:
                ln_root(p)

            def normalise(g, u):
                pool.wait_ge(farg_done, g + 1)
                seq.link(nc.gpsimd.tensor_tensor(f_r[:, u, 0, :], f_tmp[:, u, 4, :], neg_half[:, 0:GT], ALU.pow))
                seq.link(nc.gpsimd.tensor_tensor(f_r[:, u, 1, :], f_r[:, u, 0, :], f_tmp[:, u, 3, :], ALU.mult))
                for t in range(GT):
                    nc.gpsimd.tensor_scalar(g_ring[:, u, t, :], g_ring[:, u, t, :], f_r[:, u, 0, t:t + 1],
                                            f_r[:, u, 1, t:t + 1], ALU.mult, ALU.add).then_inc(z_done, 1)

            normalise(0, 0)
            pool.wait_ge(bn_arg, 1)
            nc.gpsimd.tensor_tensor(bn[:, 5, :], bn[:, 4, :], neg_half[:, 0:3], ALU.pow).then_inc(bn_pow, 1)
            normalise(1, 1)
            normalise(2, 0)
            pool.wait_ge(m_abs, 1)
            nc.gpsimd.partition_all_reduce(amax[:, 2:4], amax[:, 0:2], P, REDUCE_ABSMAX).then_inc(m_all, 1)
            for g in range(3, NG):
                normalise(g, g % 2)

            with pool.Fori(0, NG) as g:
                pool.wait_ge(fadd_done, g + 1)
                pool.wait_ge(bias_done, GT)
                nc.gpsimd.tensor_tensor(x_sb[:, bass.ds(GT * g, GT), :], x_sb[:, bass.ds(GT * g, GT), :], bias4[:],
                                        ALU.add).then_inc(badd_done, 1)

        @block.scalar
        def _(act):
            act.dma_start(lora_sb[:], lora_d[:, :]).then_inc(lora_in, 16)
            act.dma_start(w_sb[:, W_PF:], w_d[:, W_PF:]).then_inc(w_in, 16)
            act.sem_inc(exp_done, SLOTS)

            def ln_norm(g, u):
                if isinstance(g, int):
                    wait(act, ln_nb_done, g // 2 + 1)
                act.wait_ge(gram_done, g - 1 + SLOTS)
                for t in range(GT):
                    n = GT * g + t
                    nc.scalar.activation(xn_ring[:, u, t, 0:C], x_sb[:, bass.ds(n, 1), :], ACT.Identity,
                                         bias=ln_nb[:, bass.ds(n, 1)], scale=ln_r[:, bass.ds(n, 1)]).then_inc(xn_done, 1)

            def x_hi(g, u):
                act.wait_ge(xT_done, g + 1)
                nc.scalar.activation(xT_hi[:, tokens(GT * g, GT)], banks[:, 5 + u, :], ACT.Copy).then_inc(xhi_done, 1)

            ln_norm(0, 0)
            with act.Fori(0, 3) as p:
                ln_norm(2 * p + 1, 1)
                x_hi(2 * p, 0)
                act.wait_ge(ln_nb_done, p + 2)
                ln_norm(2 * p + 2, 0)
                x_hi(2 * p + 1, 1)
            ln_norm(7, 1)
            x_hi(6, 0)
            x_hi(7, 1)

            def gelus(g, u):
                for t in range(GT):
                    n = GT * g + t
                    act.wait_ge(h_done, n + 1)
                    if t == 0:
                        wait(act, zT_done, HC * (g - 1))
                    nc.scalar.activation(g_ring[:, u, t, :], banks[:, t % 2, :], ACT.Gelu,
                                         scale=1.0 / XS).then_inc(gelu_done, 1)

            def z_high(g, u):
                for c in range(HC):
                    act.wait_ge(zT_done, HC * g + c + 1)
                    if c == 0:
                        wait(act, f_done, g - 1)
                        wait(act, lnw_done, 1)
                    nc.scalar.activation(z_hi[:, u, c, :], banks[:, 2 + c % 2, :], ACT.Copy,
                                         scale=lnw_s[:, c:c + 1]).then_inc(zhi_done, 1)

            gelus(0, 0)
            gelus(1, 1)
            z_high(0, 0)
            gelus(2, 0)
            z_high(1, 1)
            act.wait_ge(m_mm, 1)
            for t in range(GT):
                nc.scalar.activation(bias4[:, t, :], banks[:, 7, 257:257 + C], ACT.Copy).then_inc(bias_done, 1)
            with act.Fori(1, 3) as p:
                gelus(2 * p + 1, 1)
                z_high(2 * p, 0)
                gelus(2 * p + 2, 0)
                z_high(2 * p + 1, 1)
            gelus(7, 1)
            z_high(6, 0)
            z_high(7, 1)

            act.wait_ge(m_split, 1)
            with act.Fori(0, NG // 2) as p:
                for u in range(2):
                    g = 2 * p + u
                    act.wait_ge(q_mm, g + 1)
                    nc.scalar.activation(qT_hi[:, tokens(GT * g, GT)], banks[:, 5 + 2 * u, :], ACT.Identity,
                                         bias=amax[:, 9:10]).then_inc(qhi_done, 1)
                    act.wait_ge(u_mm, g + 1)
                    nc.scalar.activation(u_hi[:, bass.ds(GT * g, GT), :], banks[:, 6 - 6 * u, :], ACT.Copy).then_inc(uhi_done, 1)

            def exps(b, i):
                n, par = QT * b + i, i % 2
                act.wait_ge(nb_done, n + 1)
                transposed = CHUNK0[i - 1] if i else -CHUNKS[QT - 1]
                wait(act, eT_done, BATCH_CHUNKS * b + transposed + SLOTS)
                act.wait_ge(fin_done, n - 1 + SLOTS)
                nc.scalar.activation(e_ring[:, par, 0:P * (i + 1)],
                                     banks[:, 2 * par:2 * par + 2, :].rearrange("p a n -> p (a n)")[:, 0:P * (i + 1)],
                                     ACT.Exp, bias=nbias[:, par:par + 1], scale=amax[:, 8:9],
                                     accum_out=rowsum[:, par:par + 1]).then_inc(exp_done, 1)

            def e_high(b, i):
                n, par = QT * b + i, i % 2
                act.wait_ge(pv_done, n - 1 + SLOTS)
                for k in range(CHUNKS[i]):
                    j0, j1 = GT * k, min(GT * (k + 1), i + 1)
                    act.wait_ge(eT_done, BATCH_CHUNKS * b + CHUNK0[i] + k + 1 + SLOTS)
                    nc.scalar.activation(eT_hi[:, par, j0:j1, :], banks[:, 5 + (CHUNK0[i] + k) % 2, 0:P * (j1 - j0)],
                                         ACT.Copy).then_inc(ehi_done, 1)

            exps(0, 0)

            def attend(b, last):
                for i in range(QT):
                    if i + 1 < QT:
                        exps(b, i + 1)
                    elif not last:
                        exps(b + 1, 0)
                    e_high(b, i)

            with act.Fori(0, BATCH - 1) as b:
                attend(b, False)
            attend(BATCH - 1, True)

        @block.vector
        def _(dve):
            seq = Sequence(dve, dve_seq)
            dve.sem_inc(fin_done, SLOTS)
            dve.sem_inc(elo_done, SLOTS)

            def moments(st, tmp, n, nmean, arg, count, scale, eps):
                seq.mark(nc.vector.tensor_tensor(tmp[:, 0, 0:n], st[:, :, 1], st[:, :, 4], ALU.subtract))
                seq.mark(nc.vector.tensor_tensor(tmp[:, 1, 0:n], st[:, :, 2], st[:, :, 5], ALU.add))
                seq.mark(nc.vector.tensor_tensor(tmp[:, 2, 0:n], st[:, :, 1], st[:, :, 4], ALU.add))
                seq.settle()
                seq.mark(nc.vector.tensor_tensor(tmp[:, 0, 0:n], tmp[:, 0, 0:n], tmp[:, 0, 0:n], ALU.mult))
                nm = nc.vector.tensor_scalar(nmean, tmp[:, 2, 0:n], -0.5, None, ALU.mult)
                seq.mark(nm)
                seq.settle()
                seq.link(nc.vector.scalar_tensor_tensor(tmp[:, 1, 0:n], tmp[:, 0, 0:n], count / 4.0, tmp[:, 1, 0:n],
                                                        ALU.mult, ALU.add))
                return nc.vector.tensor_scalar(arg, tmp[:, 1, 0:n], scale / count, scale * eps, ALU.mult, ALU.add)

            MOMENTS = 6

            def ln_stats(p):
                for t in range(8):
                    seq.mark(nc.vector.bn_stats(ln_st[:, bass.ds(8 * p + t, 1), :], x_sb[:, bass.ds(8 * p + t, 1), :]))
                seq.settle()
                eight = bass.ds(8 * p, 8)
                moments(ln_st[:, eight, :], ln_tmp, 8, ln_nmean[:, eight], ln_arg[:, eight], C, 1.0 / XS ** 2,
                        LN_EPS).then_inc(ln_arg_done, 1)

            LN_STATS = 8 + MOMENTS

            def ln_shift(p):
                eight = bass.ds(8 * p, 8)
                dve.wait_ge(ln_pow, p + 1)
                nc.vector.tensor_tensor(ln_nb[:, eight], ln_nmean[:, eight], ln_r[:, eight],
                                        ALU.mult).then_inc(ln_nb_done, 1)

            def x_low(g, u):
                dve.wait_ge(xhi_done, g + 1)
                nc.vector.tensor_tensor(xT_lo[:, tokens(GT * g, GT)], banks[:, 5 + u, :],
                                        xT_hi[:, tokens(GT * g, GT)], ALU.subtract).then_inc(xlo_done, 1)

            dve.wait_ge(wfc_in, 16)
            nc.vector.tensor_reduce(wabs[:, 0:1], w_sb[:, W_FC:W_FC + H], axis=AXX, op=ALU.add,
                                    apply_absolute_value=True).then_inc(wabs_done, 1)
            dve.wait_ge(x_in[0], 16)
            ln_stats(0)

            def threshold(k):
                dve.wait_ge(thr_sum, k + 1)
                seq.link(nc.vector.tensor_scalar(thr[:, 2 * k:2 * k + 1], banks[:, 4, k:k + 1], 0.5 / (H * C), 0.5 * Q_EPS,
                                                 ALU.mult, ALU.add))
                seq.link(nc.vector.tensor_scalar(thr[:, 2 * k + 1:2 * k + 2], thr[:, 2 * k:2 * k + 1], -1.0, None, ALU.mult))

            def quantise(k, src, dst):
                seq.link(nc.vector.tensor_scalar(below[:], src, thr[:, 2 * k + 1:2 * k + 2], None, ALU.is_lt))
                return nc.vector.scalar_tensor_tensor(dst, src, thr[:, 2 * k:2 * k + 1], below[:], ALU.is_gt, ALU.subtract)

            threshold(0)
            quantise(0, w_sb[:, W_FC:W_FC + H], wq_fc[:]).then_inc(wq_fc_done, 1)
            dve.wait_ge(w_in, 16)
            nc.vector.tensor_reduce(wabs[:, 1:2], w_sb[:, W_PF:W_PF + H], axis=AXX, op=ALU.add,
                                    apply_absolute_value=True).then_inc(wabs_done, 1)
            nc.vector.tensor_reduce(lnw_abs[:, 0:1], lnw_c, axis=AXX, op=ALU.max,
                                    apply_absolute_value=True).then_inc(lnw_red, 1)
            dve.wait_ge(x_in[1], 16)
            ln_stats(1)
            ln_shift(0)
            dve.wait_ge(x_in[2], 16)
            dve.wait_ge(x_in[3], 16)
            start = seq.count
            with dve.Fori(0, 2) as p:
                seq.count = start + LN_STATS * p
                ln_stats(p + 2)
                ln_shift(p + 1)
                x_low(2 * p, 0)
                x_low(2 * p + 1, 1)
            seq.count = start + 2 * LN_STATS
            ln_shift(3)
            dve.wait_ge(prep_mm, 1)
            nc.vector.tensor_tensor(wmT[:], banks[:, 0, 0:3 * C], w_sb[:, W_QKVT:W_QKVT + 3 * C], ALU.add).then_inc(prep_wm, 1)
            dve.wait_ge(prep_mm, 2)
            nc.vector.tensor_tensor(wm[:].rearrange("p j c -> p (j c)"), banks[:, 1, 0:3 * C], w_sb[:, W_QKV:W_QKV + 3 * C],
                                    ALU.add).then_inc(prep_wm, 1)
            dve.wait_ge(prep_mm, 3)
            nc.vector.tensor_tensor(woT[:], banks[:, 2, 0:C], w_sb[:, W_OT:W_OT + C], ALU.add).then_inc(woT_done, 1)
            for g in range(4, NG):
                x_low(g, g % 2)
            threshold(1)
            seq.link(quantise(1, w_sb[:, W_PF:W_PF + H], wq_pf32[:].rearrange("p k c -> p (k c)")))
            nc.vector.tensor_copy(wq_pf[:], wq_pf32[:]).then_inc(wq_pf_done, 1)
            dve.wait_ge(lnw_all, 1)
            seq.link(nc.vector.tensor_scalar(ffn_scale[:, 0:1], lnw_abs[:, 1:2], 1.0 / ZS, 1e-30, ALU.mult, ALU.max))
            seq.link(nc.vector.reciprocal(ffn_scale[:, 1:2], ffn_scale[:, 0:1]))
            nc.vector.tensor_scalar(lnw_s[:], lnw_c, ffn_scale[:, 1:2], None, ALU.mult).then_inc(lnw_done, 1)
            seq.mark(nc.vector.tensor_copy(lnb_bc[:], lnb_c.unsqueeze(2).broadcast_to([P, HC, P])))
            dve.wait_ge(gram_done, NG + SLOTS)
            nc.vector.tensor_copy(gram[:], banks[:, 7, 0:C + 1]).then_inc(gram_cp, 1)
            dve.wait_ge(two_mm, 1)
            nc.vector.tensor_copy(two_proj[:], banks[:, 3, 0:C]).then_inc(two_done, 1)

            def f_stats(g, u):
                for t in range(GT):
                    dve.wait_ge(gelu_done, GT * g + t + 1)
                    seq.mark(nc.vector.bn_stats(fst[:, u, t, :], g_ring[:, u, t, :]))
                seq.settle()
                moments(fst[:, u, :, :], f_tmp[:, u, :, :], GT, f_tmp[:, u, 3, :], f_tmp[:, u, 4, :], H, 1.0,
                        LN_EPS).then_inc(farg_done, 1)

            F_STATS = GT + MOMENTS

            def z_low(g, u):
                if isinstance(g, int) and g == 0:
                    dve.wait_ge(lnw_done, 1)
                wait(dve, f_done, g - 1)
                for c in range(HC):
                    dve.wait_ge(zhi_done, HC * g + c + 1)
                    nc.vector.scalar_tensor_tensor(z_lo[:, u, c, :], banks[:, 2 + c % 2, :], lnw_s[:, c:c + 1],
                                                   z_hi[:, u, c, :], ALU.mult, ALU.subtract).then_inc(zlo_done, 1)

            def f_add(g):
                dve.wait_ge(f_done, g + 1)
                rows = x_sb[:, bass.ds(GT * g, GT), :]
                nc.vector.scalar_tensor_tensor(rows, banks[:, 4, :].rearrange("p (t c) -> p t c", t=GT), ffn_scale[:, 0:1],
                                               rows, ALU.mult, ALU.add).then_inc(fadd_done, 1)

            f_stats(0, 0)
            dve.wait_ge(bn_z, 1)
            zb = banks[:, 5, 0:3 * (C + 1)].rearrange("p (j c) -> p j c", j=3)
            for j in range(3):
                seq.link(nc.vector.tensor_tensor_reduce(out=bn_prod[:], in0=zb[:, j, 0:C], in1=wm[:, j, :], scale=1.0, scalar=0.0,
                                                        op0=ALU.mult, op1=ALU.add, accum_out=bn[:, 0, j:j + 1]))
            seq.link(nc.vector.tensor_scalar(bn[:, 1, :], zb[:, :, C], 1.0 / (XS * TOKENS), None, ALU.mult))
            seq.link(nc.vector.tensor_tensor(bn[:, 2, :], bn[:, 1, :], bn[:, 1, :], ALU.mult))
            seq.link(nc.vector.scalar_tensor_tensor(bn[:, 3, :], bn[:, 0, :], 1.0 / (XS * XS * TOKENS), bn[:, 2, :],
                                                    ALU.mult, ALU.subtract))
            nc.vector.tensor_scalar(bn[:, 4, :], bn[:, 3, :], 0.0, BN_EPS, ALU.max, ALU.add).then_inc(bn_arg, 1)
            f_stats(1, 1)
            dve.wait_ge(bn_pow, 1)
            seq.link(nc.vector.tensor_tensor(bn[:, 6, :], gamma_c, bn[:, 5, :], ALU.mult))
            seq.link(nc.vector.tensor_tensor(bn[:, 7, :], bn[:, 1, :], bn[:, 6, :], ALU.mult))
            seq.link(nc.vector.tensor_tensor(bn[:, 8, :], beta_c, bn[:, 7, :], ALU.subtract))
            seq.mark(nc.vector.tensor_tensor(bn[:, 9, 0:1], bn[:, 6, 0:1], bn[:, 6, 1:2], ALU.mult))
            nc.vector.tensor_tensor(bn[:, 10, 0:1], bn[:, 8, 0:1], bn[:, 6, 1:2], ALU.mult).then_inc(bn_w, 1)
            nc.vector.tensor_scalar(wv_scaled[:], wm[:, 2, :], bn[:, 6, 2:3], None, ALU.mult).then_inc(bn_w, 1)
            nc.vector.tensor_copy(bv_bc[:], bn[:, 8, 2:3].broadcast_to([P, P])).then_inc(bn_w, 1)
            seq.settle()
            nc.vector.tensor_scalar(wq_scaled[:], wm[:, 0, :], bn[:, 9, 0:1], None, ALU.mult).then_inc(bn_w, 1)
            z_low(0, 0)
            f_add(0)
            dve.wait_ge(m_mm, 1)
            seq.mark(nc.vector.tensor_copy(m_f[:], banks[:, 7, 0:C + 1]))
            seq.mark(nc.vector.tensor_copy(u_f[:], banks[:, 7, C + 1:2 * C + 1]))
            seq.settle()
            seq.mark(nc.vector.tensor_reduce(amax[:, 0:1], m_f[:], axis=AXX, op=ALU.max, apply_absolute_value=True))
            seq.mark(nc.vector.tensor_reduce(amax[:, 1:2], u_f[:], axis=AXX, op=ALU.max, apply_absolute_value=True))
            seq.settle()
            nc.vector.tensor_copy(amax[:, 0:2], amax[:, 0:2]).then_inc(m_abs, 1)
            f_stats(2, 0)
            z_low(1, 1)
            f_add(1)
            dve.wait_ge(m_all, 1)
            seq.mark(nc.vector.tensor_scalar(amax[:, 4:5], amax[:, 2:3], 1.0, 1.0 / MS, ALU.max, ALU.mult))
            seq.mark(nc.vector.tensor_scalar(amax[:, 5:6], amax[:, 3:4], 1e-30, 1.0 / MS, ALU.max, ALU.mult))
            seq.settle()
            seq.mark(nc.vector.reciprocal(amax[:, 6:8], amax[:, 4:6]))
            seq.mark(nc.vector.tensor_scalar(amax[:, 8:9], amax[:, 4:5], float(C) ** -0.5 / (XS * XS), None, ALU.mult))
            seq.settle()
            seq.mark(nc.vector.tensor_scalar(m_f[:], m_f[:], amax[:, 6:7], None, ALU.mult))
            seq.mark(nc.vector.tensor_scalar(u_f[:], u_f[:], amax[:, 7:8], None, ALU.mult))
            seq.settle()
            seq.mark(nc.vector.tensor_copy(m_hi[:], m_f[:, 0:C]))
            seq.mark(nc.vector.tensor_copy(u_hi_w[:], u_f[:]))
            seq.mark(nc.vector.tensor_scalar(amax[:, 9:10], m_f[:, C:C + 1], XS, None, ALU.mult))
            seq.mark(nc.vector.tensor_scalar(amax[:, 7:8], amax[:, 5:6], 1.0 / XS, None, ALU.mult))
            seq.settle()
            seq.link(nc.vector.tensor_tensor(m_lo[:], m_f[:, 0:C], m_hi[:], ALU.subtract))
            nc.vector.tensor_tensor(u_lo_w[:], u_f[:], u_hi_w[:], ALU.subtract).then_inc(m_split, 1)

            start = seq.count
            with dve.Fori(1, 3) as p:
                seq.count = start + 2 * F_STATS * (p - 1)
                f_stats(2 * p + 1, 1)
                z_low(2 * p, 0)
                f_add(2 * p)
                f_stats(2 * p + 2, 0)
                z_low(2 * p + 1, 1)
                f_add(2 * p + 1)
            seq.count = start + 4 * F_STATS
            f_stats(7, 1)
            z_low(6, 0)
            f_add(6)
            z_low(7, 1)
            f_add(7)

            with dve.Fori(0, NG // 2) as p:
                for u in range(2):
                    g = 2 * p + u
                    dve.wait_ge(qhi_done, g + 1)
                    nc.vector.scalar_tensor_tensor(qT_lo[:, tokens(GT * g, GT)], banks[:, 5 + 2 * u, :], amax[:, 9:10],
                                                   qT_hi[:, tokens(GT * g, GT)], ALU.add, ALU.subtract).then_inc(qlo_done, 1)
                    dve.wait_ge(uhi_done, g + 1)
                    nc.vector.tensor_tensor(u_lo[:, bass.ds(GT * g, GT), :],
                                            banks[:, 6 - 6 * u, :].rearrange("p (t c) -> p t c", t=GT),
                                            u_hi[:, bass.ds(GT * g, GT), :], ALU.subtract).then_inc(ulo_done, 1)

            def row_max(b, i):
                n, par = QT * b + i, i % 2
                dve.wait_ge(s_done, n + 1)
                dve.wait_ge(exp_done, n - 1 + SLOTS)
                seq.link(nc.vector.tensor_reduce(
                    nmax[:, par:par + 1],
                    banks[:, 2 * par:2 * par + 2, :].rearrange("p a n -> p (a n)")[:, 0:P * (i + 1)],
                    axis=AXX, op=ALU.max, negate=True))
                nc.vector.tensor_scalar(nbias[:, par:par + 1], nmax[:, par:par + 1], amax[:, 8:9], LN_PS,
                                        ALU.mult, ALU.add).then_inc(nb_done, 1)

            def e_low(b, i):
                n, par = QT * b + i, i % 2
                dve.wait_ge(pv_done, n - 1 + SLOTS)
                for k in range(CHUNKS[i]):
                    j0, j1 = GT * k, min(GT * (k + 1), i + 1)
                    dve.wait_ge(ehi_done, BATCH_CHUNKS * b + CHUNK0[i] + k + 1)
                    nc.vector.tensor_tensor(eT_lo[:, par, j0:j1, :].rearrange("p j t -> p (j t)"),
                                            banks[:, 5 + (CHUNK0[i] + k) % 2, 0:P * (j1 - j0)],
                                            eT_hi[:, par, j0:j1, :].rearrange("p j t -> p (j t)"),
                                            ALU.subtract).then_inc(elo_done, 1)

            def finish(b, i):
                n, par = QT * b + i, i % 2
                dve.wait_ge(exp_done, n + 1 + SLOTS)
                seq.link(nc.vector.reciprocal(rinv[:, par, 0:1], rowsum[:, par:par + 1]))
                seq.link(nc.vector.tensor_scalar(rinv[:, par, 1:2], rinv[:, par, 0:1], amax[:, 7:8], None, ALU.mult))
                dve.wait_ge(pv_done, n + 1 + SLOTS)
                dve.wait_ge(badd_done, 2 * b + i // GT + 1)
                row = x_sb[:, bass.ds(n, 1), :].rearrange("p o c -> p (o c)")
                nc.vector.scalar_tensor_tensor(row, banks[:, 4 + 3 * par, 0:C], rinv[:, par, 1:2], row,
                                               ALU.mult, ALU.add).then_inc(fin_done, 1)

            row_max(0, 0)
            row_max(0, 1)
            e_low(0, 0)

            def attend(b, last):
                for i in range(QT):
                    if i + 2 < QT:
                        row_max(b, i + 2)
                    elif not last:
                        row_max(b + 1, i + 2 - QT)
                    finish(b, i)
                    if i + 1 < QT:
                        e_low(b, i + 1)
                    elif not last:
                        e_low(b + 1, 0)

            start = seq.count
            with dve.Fori(0, BATCH - 1) as b:
                seq.count = start + 3 * QT * b
                attend(b, False)
            seq.count = start + 3 * QT * (BATCH - 1)
            attend(BATCH - 1, True)

        @block.tensor
        def _(pe):
            mm = nc.tensor.matmul
            pe.sem_inc(gram_done, SLOTS)
            pe.sem_inc(eT_done, SLOTS)
            pe.sem_inc(pv_done, SLOTS)
            pe.wait_ge(consts, 1)
            pe.wait_ge(wabs_done, 1)
            mm(banks[:, 4, 0:1], ones[:], wabs[:, 0:1], start=True, stop=True).then_inc(thr_sum, 1)

            def ln_products(g, u, first):
                pe.wait_ge(xn_done, GT * (g + 1))
                wait(pe, xlo_done, g - 1)
                for t in range(GT):
                    last = nc.tensor.transpose(banks[:, 5 + u, tokens(t)], xn_ring[:, u, t, 0:C], ident[:])
                last.then_inc(xT_done, 1)
                for t in range(GT):
                    last = mm(banks[:, 7, 0:C + 1], xn_ring[:, u, t, 0:C], xn_ring[:, u, t, :], start=(first and t == 0),
                              stop=(isinstance(g, int) and g == NG - 1 and t == GT - 1))
                last.then_inc(gram_done, 1)

            pe.wait_ge(consts, 3)
            ln_products(0, 0, True)
            ln_products(1, 1, False)
            pe.wait_ge(consts, 8)
            pe.wait_ge(lora_in, 16)
            for m in range(3):
                last = mm(banks[:, 0, 0:3 * C], lora_sb[:, L_B + C * m:L_B + C * (m + 1)], az[:, m, :],
                          start=(m == 0), stop=(m == 2))
            last.then_inc(prep_mm, 1)
            for j in range(3):
                for m in range(3):
                    last = mm(banks[:, 1, C * j:C * (j + 1)], az[:, m, C * j:C * (j + 1)],
                              lora_sb[:, L_B + C * m:L_B + C * (m + 1)], start=(m == 0), stop=(m == 2))
            last.then_inc(prep_mm, 1)
            mm(banks[:, 2, 0:C], lora_sb[:, L_PB:L_PB + C], lora_sb[:, L_PAT:L_PAT + C], start=True, stop=True)\
                .then_inc(prep_mm, 1)
            pe.wait_ge(wabs_done, 2)
            mm(banks[:, 4, 0:2], ones[:], wabs[:, 0:2], start=True, stop=True).then_inc(thr_sum, 1)
            with pe.Fori(1, 3) as p:
                ln_products(2 * p, 0, False)
                ln_products(2 * p + 1, 1, False)
            ln_products(6, 0, False)
            ln_products(7, 1, False)
            pe.wait_ge(woT_done, 1)
            mm(banks[:, 3, 0:C], w_sb[:, W_O:W_O + C], woT[:], start=True, stop=True).then_inc(two_mm, 1)
            pe.wait_ge(wq_fc_done, 1)

            def ffn_up(g):
                for t in range(GT):
                    n = GT * g + t
                    wait(pe, gelu_done, n - 1)
                    mm(banks[:, t % 2, :], xT_hi[:, tokens(n)], wq_fc[:], start=True, stop=False)
                    mm(banks[:, t % 2, :], xT_lo[:, tokens(n)], wq_fc[:], start=False, stop=True).then_inc(h_done, 1)

            def ffn_down(g, u):
                pe.wait_ge(z_done, GT * (g + 1))
                for c in range(HC):
                    wait(pe, zlo_done, HC * g + c - 1)
                    for t in range(GT):
                        last = nc.tensor.transpose(banks[:, 2 + c % 2, tokens(t)], g_ring[:, u, t, tokens(c)], ident[:])
                    last.then_inc(zT_done, 1)
                pe.wait_ge(zlo_done, HC * (g + 1))
                wait(pe, fadd_done, g)
                for t in range(GT):
                    for c in range(HC):
                        mm(banks[:, 4, tokens(t)], z_hi[:, u, c, tokens(t)], wq_pf[:, c, :], start=(c == 0), stop=False)
                        last = mm(banks[:, 4, tokens(t)], z_lo[:, u, c, tokens(t)], wq_pf[:, c, :],
                                  start=False, stop=(c == HC - 1))
                last.then_inc(f_done, 1)

            pe.wait_ge(xlo_done, NG)
            pe.wait_ge(prep_wm, 2)
            ffn_up(0)
            pe.wait_ge(gram_cp, 1)
            for j in range(3):
                last = mm(banks[:, 5, (C + 1) * j:(C + 1) * (j + 1)], wmT[:, C * j:C * (j + 1)], gram[:], start=True, stop=True)
            last.then_inc(bn_z, 1)
            ffn_up(1)
            pe.wait_ge(wq_pf_done, 1)
            pe.wait_ge(two_done, 1)
            ffn_down(0, 0)
            pe.wait_ge(bn_w, 4)
            mm(banks[:, 7, 0:C], wq_scaled[:], wm[:, 1, :], start=True, stop=True)
            mm(banks[:, 7, C:C + 1], wm[:, 1, :], bn[:, 10, 0:1], start=True, stop=True)
            mm(banks[:, 7, C + 1:2 * C + 1], wv_scaled[:], two_proj[:], start=True, stop=True)
            mm(banks[:, 7, 257:257 + C], bv_bc[:], two_proj[:], start=True, stop=False)
            for c in range(HC):
                last = mm(banks[:, 7, 257:257 + C], lnb_bc[:, c, :], wq_pf32[:, c, :], start=False, stop=(c == HC - 1))
            last.then_inc(m_mm, 1)
            ffn_up(2)
            ffn_down(1, 1)
            with pe.Fori(1, 3) as p:
                ffn_up(2 * p + 1)
                ffn_down(2 * p, 0)
                ffn_up(2 * p + 2)
                ffn_down(2 * p + 1, 1)
            ffn_up(7)
            ffn_down(6, 0)
            ffn_down(7, 1)

            pe.wait_ge(m_split, 1)
            pe.wait_ge(bias_done, GT)
            with pe.Fori(0, NG // 2) as p:
                for u in range(2):
                    g = 2 * p + u
                    if u == 0:
                        pe.wait_ge(fadd_done, NG)
                    xs = tokens(GT * g, GT)
                    q_bank = banks[:, 5 + 2 * u, :]
                    if u == 1:
                        pe.wait_ge(qlo_done, 2 * p + 1)
                        pe.wait_ge(ulo_done, 2 * p + 1)
                    mm(q_bank, m_hi[:], xT_hi[:, xs], start=True, stop=False)
                    mm(q_bank, m_hi[:], xT_lo[:, xs], start=False, stop=False)
                    mm(q_bank, m_lo[:], xT_hi[:, xs], start=False, stop=True).then_inc(q_mm, 1)
                    for t in range(GT):
                        n, to = GT * g + t, banks[:, 6 - 6 * u, tokens(t)]
                        mm(to, xT_hi[:, tokens(n)], u_hi_w[:], start=True, stop=False)
                        mm(to, xT_hi[:, tokens(n)], u_lo_w[:], start=False, stop=False)
                        last = mm(to, xT_lo[:, tokens(n)], u_hi_w[:], start=False, stop=True)
                    last.then_inc(u_mm, 1)
            pe.wait_ge(qlo_done, NG)
            pe.wait_ge(ulo_done, NG)

            def scores(b, i):
                n, par = QT * b + i, i % 2
                pe.wait_ge(exp_done, n - 1 + SLOTS)
                for k in range(CHUNKS[i]):
                    lo, hi = 512 * k, min(512 * (k + 1), P * (i + 1))
                    to, keys = banks[:, 2 * par + k, 0:hi - lo], bass.ds(T * b + lo, hi - lo)
                    diagonal = k == CHUNKS[i] - 1
                    mm(to, qT_hi[:, tokens(n)], xT_hi[:, keys], start=True, stop=False)
                    mm(to, qT_hi[:, tokens(n)], xT_lo[:, keys], start=False, stop=False)
                    last = mm(to, qT_lo[:, tokens(n)], xT_hi[:, keys], start=False, stop=not diagonal)
                    if diagonal:
                        last = mm(banks[:, 2 * par + k, hi - lo - P:hi - lo], ident_bf[:], mask_bf[:], start=False, stop=True)
                last.then_inc(s_done, 1)

            def transpose_probs(b, i):
                n, par = QT * b + i, i % 2
                pe.wait_ge(exp_done, n + 1 + SLOTS)
                for k in range(CHUNKS[i]):
                    pe.wait_ge(elo_done, BATCH_CHUNKS * b + CHUNK0[i] + k - 1 + SLOTS)
                    for j in range(GT * k, min(GT * (k + 1), i + 1)):
                        last = nc.tensor.transpose(banks[:, 5 + (CHUNK0[i] + k) % 2, tokens(j - GT * k)],
                                                   e_ring[:, par, tokens(j)], ident[:])
                    last.then_inc(eT_done, 1)

            def attend_values(b, i):
                n, par = QT * b + i, i % 2
                pe.wait_ge(elo_done, BATCH_CHUNKS * b + CHUNK0[i] + CHUNKS[i] + SLOTS)
                pe.wait_ge(fin_done, n - 1 + SLOTS)
                to = banks[:, 4 + 3 * par, 0:C]
                for j in range(i + 1):
                    vh = u_hi[:, bass.ds(QT * b + j, 1), :].rearrange("p o c -> p (o c)")
                    vl = u_lo[:, bass.ds(QT * b + j, 1), :].rearrange("p o c -> p (o c)")
                    mm(to, eT_hi[:, par, j, :], vh, start=(j == 0), stop=False)
                    mm(to, eT_hi[:, par, j, :], vl, start=False, stop=False)
                    last = mm(to, eT_lo[:, par, j, :], vh, start=False, stop=(j == i))
                last.then_inc(pv_done, 1)

            scores(0, 0)
            scores(0, 1)
            transpose_probs(0, 0)

            def attend(b, last):
                for i in range(QT):
                    if i + 2 < QT:
                        scores(b, i + 2)
                    elif not last:
                        scores(b + 1, i + 2 - QT)
                    attend_values(b, i)
                    if i + 1 < QT:
                        transpose_probs(b, i + 1)
                    elif not last:
                        transpose_probs(b + 1, 0)

            with pe.Fori(0, BATCH - 1) as b:
                attend(b, False)
            attend(BATCH - 1, True)


def kernel(L0_attn_x, L0_attn_W_attn, L0_attn_W_proj, L0_attn_lora_attn_A, L0_attn_lora_attn_B, L0_attn_lora_proj_A,
           L0_attn_lora_proj_B, L0_attn_bn_gamma, L0_attn_bn_beta, L0_ffn_W_fc, L0_ffn_ln_w, L0_ffn_ln_b, L0_ffn_W_proj):
    import numpy as np
    import concourse.bacc as bacc
    from concourse.bass_utils import run_bass_kernel_spmd

    def rows_to_partitions(a):
        return a.reshape(-1, P, a.shape[-1]).transpose(1, 0, 2).reshape(P, -1)

    a = {k: np.asarray(v) for k, v in dict(
        x=L0_attn_x, wa=L0_attn_W_attn, wo=L0_attn_W_proj, aA=L0_attn_lora_attn_A, aB=L0_attn_lora_attn_B,
        pA=L0_attn_lora_proj_A, pB=L0_attn_lora_proj_B, gamma=L0_attn_bn_gamma, beta=L0_attn_bn_beta, fc=L0_ffn_W_fc,
        lw=L0_ffn_ln_w, lb=L0_ffn_ln_b, pf=L0_ffn_W_proj).items()}
    weights = np.concatenate([
        a["fc"].T, rows_to_partitions(a["pf"].T), rows_to_partitions(a["wa"]), a["wa"].T, a["wo"], a["wo"].T,
        a["lw"].reshape(HC, P).T, a["lb"].reshape(HC, P).T, a["gamma"].reshape(3, P).T, a["beta"].reshape(3, P).T], axis=1)
    lora = np.concatenate([a["aA"].T, a["aB"], a["pA"].T, a["pB"]], axis=1)

    nc = bacc.Bacc("TRN2", target_bir_lowering=False, num_devices=1)
    arrays = {"x_dram": np.ascontiguousarray(a["x"]), "w_dram": np.ascontiguousarray(weights),
              "lora_dram": np.ascontiguousarray(lora)}
    ins = [nc.dram_tensor(n, v.shape, mybir.dt.from_np(v.dtype), kind="ExternalInput").ap() for n, v in arrays.items()]
    out = nc.dram_tensor("out_dram", a["x"].shape, F32, kind="ExternalOutput").ap()
    block_kernel(nc, *ins, out)
    r = run_bass_kernel_spmd(nc, [arrays], core_ids=[0])
    return r.results[0]["out_dram"]
```

```python
from contextlib import ExitStack

import concourse.bass as bass
from concourse import mybir

F32, F16, BF16 = mybir.dt.float32, mybir.dt.float16, mybir.dt.bfloat16
ALU = mybir.AluOpType
ACT = mybir.ActivationFunctionType
AXX = mybir.AxisListType.X
REDUCE_ABSMAX = bass.bass_isa.ReduceOp.absmax

P = 128
BATCH, T, C, R, H = 4, 1024, 128, 64, 512
TOKENS = BATCH * T
NT = TOKENS // P
GT = 4
NG = NT // GT
QT = T // P
HC = H // P
LN_EPS, BN_EPS, Q_EPS = 1e-5, 1e-5, 1e-6

XS = 16.0
MS = 16.0
ZS = 64.0
ES = 4096.0
SLOTS = 2
MASKED = -float(2 ** 36)

ORDER = [0, 1, 2, 3, 4, 5, 6, 7]
CHUNKS = [1 if i < GT else 2 for i in ORDER]
CHUNK0 = [sum(CHUNKS[:k]) for k in range(QT)]
BATCH_CHUNKS = sum(CHUNKS)

W_FC, W_PF, W_QKV, W_QKVT, W_O, W_OT, W_COLS = 0, 512, 1024, 1408, 1792, 1920, 2048
N_COLS = 2 * HC + 6
L_AT, L_B, L_PAT, L_PB, L_END = 0, 128, 512, 640, 768


def block_kernel(nc, x_d, w_d, lora_d, out_d):
    x_v = x_d.rearrange("b (n p) c -> p (b n) c", p=P)
    out_v = out_d.rearrange("b (n p) c -> p (b n) c", p=P)
    with ExitStack() as ctx:
        def sb(name, shape, dt=F32):
            return ctx.enter_context(nc.sbuf_tensor(name, shape, dt))

        def sem(name):
            return ctx.enter_context(nc.semaphore(name))

        x_sb = sb("x_sb", [P, NT, C])
        w_sb = sb("w_sb", [P, W_COLS + N_COLS])
        lora_sb = sb("lora_sb", [R, L_END])
        ident = sb("ident", [P, P])
        ident_bf = sb("ident_bf", [P, P], BF16)
        mask_bf = sb("mask_bf", [P, P], BF16)
        ones = sb("ones", [P, P])
        az = sb("az", [R, 3, 3 * C])
        neg_half = sb("neg_half", [P, 2 * GT])
        xn_ring = sb("xn_ring", [P, 2, GT, C + 1])
        xT_hi = sb("xT_hi", [P, TOKENS], F16)
        xT_lo = sb("xT_lo", [P, TOKENS], F16)
        ln_st = sb("ln_st", [P, NT, 6])
        ln_tmp = sb("ln_tmp", [P, 3, NT])
        ln_nmean = sb("ln_nmean", [P, NT])
        ln_arg = sb("ln_arg", [P, NT])
        ln_r = sb("ln_r", [P, NT])
        ln_nb = sb("ln_nb", [P, NT])
        wabs = sb("wabs", [P, 2])
        thr = sb("thr", [P, 4])
        abs_junk = sb("abs_junk", [P, H])
        below = sb("below", [P, H], F16)
        wq_fc = sb("wq_fc", [P, H], F16)
        wq_pf = sb("wq_pf", [P, HC, C], F16)
        wq_pf32 = sb("wq_pf32", [P, HC, C])
        lnb_bc = sb("lnb_bc", [P, HC, P])
        lnw_abs = sb("lnw_abs", [P, 2])
        lnw_s = sb("lnw_s", [P, HC])
        ffn_scale = sb("ffn_scale", [P, 2])
        wm = sb("wm", [P, 3, C])
        wmT = sb("wmT", [P, 3 * C])
        woT = sb("woT", [P, C])
        two_proj = sb("two_proj", [P, C])
        gram = sb("gram", [P, C + 1])
        bn_prod = sb("bn_prod", [P, C])
        bn = sb("bn", [P, 14, 3])
        wq_scaled = sb("wq_scaled", [P, C])
        wv_scaled = sb("wv_scaled", [P, C])
        bv_bc = sb("bv_bc", [P, P])
        amax = sb("amax", [P, 10])
        m_f = sb("m_f", [P, C + 1])
        u_f = sb("u_f", [P, C])
        m_hi = sb("m_hi", [P, C], F16)
        m_lo = sb("m_lo", [P, C], F16)
        u_hi_w = sb("u_hi_w", [P, C], F16)
        u_lo_w = sb("u_lo_w", [P, C], F16)
        bias4 = sb("bias4", [P, GT, C])
        g_ring = sb("g_ring", [P, 2, GT, H])
        fst = sb("fst", [P, 2, GT, 6])
        f_mv = sb("f_mv", [P, 2, GT, 2])
        f_arg = sb("f_arg", [P, 2, 2, GT])
        f_r = sb("f_r", [P, 2, 2, GT])
        f_out = sb("f_out", [P, 2, GT * C])
        z_hi = sb("z_hi", [P, 2, HC, GT * P], F16)
        z_lo = sb("z_lo", [P, 2, HC, GT * P], F16)
        qT_hi = sb("qT_hi", [P, TOKENS], F16)
        qT_lo = sb("qT_lo", [P, TOKENS], F16)
        u_hi = sb("u_hi", [P, NT, C], F16)
        u_lo = sb("u_lo", [P, NT, C], F16)
        e_ring = sb("e_ring", [P, 2, T])
        eT_hi = sb("eT_hi", [P, 2, QT, P], F16)
        eT_lo = sb("eT_lo", [P, 2, QT, P], F16)
        nmax = sb("nmax", [P, 2])
        nbias = sb("nbias", [P, 2])
        rowsum = sb("rowsum", [P, 4])
        rowsum_s = sb("rowsum_s", [P, 4])
        rinv = sb("rinv", [P, 4])

        banks = ctx.enter_context(nc.psum_tensor("banks", [P, 8, 512], F32))

        cols = w_sb[:, W_COLS:W_COLS + N_COLS]
        lnw_c, lnb_c = cols[:, 0:HC], cols[:, HC:2 * HC]
        gamma_c, beta_c = cols[:, 2 * HC:2 * HC + 3], cols[:, 2 * HC + 3:2 * HC + 6]

        x_in = [sem(f"x_in{k}") for k in range(4)]
        wfc_in, w_in, lora_in = sem("wfc_in"), sem("w_in"), sem("lora_in")
        consts = sem("consts")
        dve_seq = sem("dve_seq")
        pool_seq = sem("pool_seq")
        wabs_done, thr_sum = sem("wabs_done"), sem("thr_sum")
        wq_fc_done, wq_pf_done = sem("wq_fc_done"), sem("wq_pf_done")
        ln_stats_done, ln_nmean_done, fneg_done = sem("ln_stats_done"), sem("ln_nmean_done"), sem("fneg_done")
        ln_arg_done, ln_nb_done = sem("ln_arg_done"), sem("ln_nb_done")
        xn_act, xn_pool, xT_done, xhi_done, xlo_done, gram_done = (
            sem("xn_act"), sem("xn_pool"), sem("xT_done"), sem("xhi_done"), sem("xlo_done"), sem("gram_done"))
        prep_mm, prep_wm, woT_done, two_mm, two_done = (
            sem("prep_mm"), sem("prep_wm"), sem("woT_done"), sem("two_mm"), sem("two_done"))
        lnw_red, lnw_all, lnw_done = sem("lnw_red"), sem("lnw_all"), sem("lnw_done")
        h_done, gelu_done, farg_done = sem("h_done"), sem("gelu_done"), sem("farg_done")
        fr_done, z_pool, z_act = sem("fr_done"), sem("z_pool"), sem("z_act")
        zT_done, zhi_done, zlo_done, f_done, fout_done, fadd_done = (
            sem("zT_done"), sem("zhi_done"), sem("zlo_done"), sem("f_done"), sem("fout_done"), sem("fadd_done"))
        gram_cp, bn_z, bn_arg, bn_pow, bn_w, m_mm = (
            sem("gram_cp"), sem("bn_z"), sem("bn_arg"), sem("bn_pow"), sem("bn_w"), sem("m_mm"))
        m_abs, m_all, m_split, bias_done = sem("m_abs"), sem("m_all"), sem("m_split"), sem("bias_done")
        q_mm, qhi_done, qlo_done = sem("q_mm"), sem("qhi_done"), sem("qlo_done")
        u_mm, uhi_done, ulo_done, badd_done = sem("u_mm"), sem("uhi_done"), sem("ulo_done"), sem("badd_done")
        max_done, sum_done = sem("max_done"), sem("sum_done")
        s_done, nb_done, exp_done, eT_done, ehi_done, elo_done, pv_done, fin_done = (
            sem("s_done"), sem("nb_done"), sem("exp_done"), sem("eT_done"), sem("ehi_done"),
            sem("elo_done"), sem("pv_done"), sem("fin_done"))
        out_done = sem("out_done")

        block = ctx.enter_context(nc.Block())

        def wait(eng, semaphore, value):
            if not isinstance(value, int) or value > 0:
                eng.wait_ge(semaphore, value)

        class Sequence:

            def __init__(self, eng, semaphore):
                self.eng, self.semaphore, self.count = eng, semaphore, 0

            def mark(self, instruction):
                instruction.then_inc(self.semaphore, 1)
                self.count = self.count + 1

            def settle(self):
                self.eng.wait_ge(self.semaphore, self.count)

            def link(self, instruction):
                self.mark(instruction)
                self.settle()

        def tokens(n, k=1):
            return bass.ds(n * P, k * P)

        @block.sync
        def _(sp):
            for k in range(4):
                if k == 1:
                    sp.dma_start(w_sb[:, W_FC:W_PF], w_d[:, W_FC:W_PF]).then_inc(wfc_in, 16)
                sp.dma_start(x_sb[:, 8 * k:8 * k + 8, :], x_v[:, 8 * k:8 * k + 8, :]).then_inc(x_in[k], 16)
            with sp.Fori(0, BATCH) as b:
                for k in range(QT):
                    row = bass.ds(QT * b + ORDER[k], 1)
                    sp.wait_ge(fin_done, QT * b + k + 1 + SLOTS)
                    sp.dma_start(out_v[:, row, :], x_sb[:, row, :]).then_inc(out_done, 16)
            sp.wait_ge(out_done, 16 * NT)

        @block.gpsimd
        def _(pool):
            seq = Sequence(pool, pool_seq)
            nc.gpsimd.memset(ones[:], 1.0).then_inc(consts, 1)
            seq.mark(nc.gpsimd.memset(neg_half[:], -0.5))
            seq.mark(nc.gpsimd.memset(ident[:], 0.0))
            seq.mark(nc.gpsimd.memset(ident_bf[:], 0.0))
            seq.mark(nc.gpsimd.memset(mask_bf[:], 0.0))
            seq.mark(nc.gpsimd.memset(az[:], 0.0))
            seq.settle()
            nc.gpsimd.affine_select(out=ident[:], in_=ident[:], compare_op=ALU.not_equal, fill=1.0,
                                    base=0, pattern=[[-1, P]], channel_multiplier=1).then_inc(consts, 1)
            nc.gpsimd.memset(xn_ring[:, :, :, C:C + 1], 1.0).then_inc(consts, 1)
            nc.gpsimd.affine_select(out=ident_bf[:], in_=ident_bf[:], compare_op=ALU.not_equal, fill=1.0,
                                    base=0, pattern=[[-1, P]], channel_multiplier=1).then_inc(consts, 1)
            nc.gpsimd.affine_select(out=mask_bf[:], in_=mask_bf[:], compare_op=ALU.is_ge, fill=MASKED,
                                    base=0, pattern=[[-1, P]], channel_multiplier=1).then_inc(consts, 1)
            pool.wait_ge(lora_in, 16)
            for m in range(3):
                spread = az[:, m, :].rearrange("r (i three) -> r i three", three=3)[:, :, m]
                nc.gpsimd.tensor_copy(spread, lora_sb[:, L_AT:L_AT + C]).then_inc(consts, 1)

            def ln_norm(p):
                eight = slice(8 * p, 8 * p + 8)
                pool.wait_ge(ln_arg_done, p + 1)
                seq.link(nc.gpsimd.tensor_tensor(ln_r[:, eight], ln_arg[:, eight], neg_half[:], ALU.pow))
                nc.gpsimd.tensor_tensor(ln_nb[:, eight], ln_nmean[:, eight], ln_r[:, eight],
                                        ALU.mult).then_inc(ln_nb_done, 1)
                pool.wait_ge(ln_nb_done, p + 1)
                for u in range(2):
                    g = 2 * p + u
                    wait(pool, gram_done, g - 1)
                    for t in range(2, GT):
                        n = GT * g + t
                        nc.gpsimd.tensor_scalar(xn_ring[:, u, t, 0:C], x_sb[:, n, :], ln_r[:, n:n + 1],
                                                ln_nb[:, n:n + 1], ALU.mult, ALU.add).then_inc(xn_pool, 1)

            ln_norm(0)
            ln_norm(1)
            ln_norm(2)
            pool.wait_ge(lnw_red, 1)
            nc.gpsimd.partition_all_reduce(lnw_abs[:, 1:2], lnw_abs[:, 0:1], P, REDUCE_ABSMAX).then_inc(lnw_all, 1)
            ln_norm(3)

            def normalise(g, u):
                for half in range(2):
                    two = slice(2 * half, 2 * half + 2)
                    pool.wait_ge(farg_done, 2 * g + half + 1)
                    seq.link(nc.gpsimd.tensor_tensor(f_r[:, u, 0, two], f_arg[:, u, 0, two], neg_half[:, 0:2], ALU.pow))
                    nc.gpsimd.tensor_tensor(f_r[:, u, 1, two], f_r[:, u, 0, two], f_arg[:, u, 1, two],
                                            ALU.mult).then_inc(fr_done, 1)
                    pool.wait_ge(fr_done, 2 * g + half + 1)
                    for t in range(2 * half, 2 if half == 0 else 3):
                        nc.gpsimd.tensor_scalar(g_ring[:, u, t, :], g_ring[:, u, t, :], f_r[:, u, 0, t:t + 1],
                                                f_r[:, u, 1, t:t + 1], ALU.mult, ALU.add).then_inc(z_pool, 1)

            def f_add(g):
                pool.wait_ge(fout_done, g + 1)
                rows = x_sb[:, GT * g:GT * (g + 1), :].rearrange("p t c -> p (t c)")
                nc.gpsimd.tensor_tensor(rows, rows, f_out[:, g % 2, :], ALU.add).then_inc(fadd_done, 1)

            for g in range(NG):
                normalise(g, g % 2)
                if g == 0:
                    pool.wait_ge(bn_arg, 1)
                    nc.gpsimd.tensor_tensor(bn[:, 5, :], bn[:, 4, :], neg_half[:, 0:3], ALU.pow).then_inc(bn_pow, 1)
                if g == 2:
                    pool.wait_ge(m_abs, 1)
                    nc.gpsimd.partition_all_reduce(amax[:, 2:4], amax[:, 0:2], P, REDUCE_ABSMAX).then_inc(m_all, 1)
                if g >= 2:
                    f_add(g - 2)
            f_add(NG - 2)
            f_add(NG - 1)

            with pool.Fori(0, NG) as g:
                pool.wait_ge(fadd_done, g + 1)
                pool.wait_ge(bias_done, GT)
                nc.gpsimd.tensor_tensor(x_sb[:, bass.ds(GT * g, GT), :], x_sb[:, bass.ds(GT * g, GT), :], bias4[:],
                                        ALU.add).then_inc(badd_done, 1)

            def exp_bias(b, k):
                n, par = QT * b + k, k % 2
                pool.wait_ge(max_done, n + 1)
                nc.gpsimd.tensor_tensor(nbias[:, par:par + 1], nmax[:, par:par + 1], amax[:, 8:9],
                                        ALU.mult).then_inc(nb_done, 1)

            def scale_sum(b, k):
                n, slot = QT * b + k, k % 4
                pool.wait_ge(exp_done, n + 1 + SLOTS)
                nc.gpsimd.tensor_tensor(rowsum_s[:, slot:slot + 1], rowsum[:, slot:slot + 1], amax[:, 7:8],
                                        ALU.mult).then_inc(sum_done, 1)

            exp_bias(0, 0)
            exp_bias(0, 1)

            def attend(b, last):
                for k in range(QT):
                    scale_sum(b, k)
                    if k + 2 < QT:
                        exp_bias(b, k + 2)
                    elif not last:
                        exp_bias(b + 1, k + 2 - QT)

            with pool.Fori(0, BATCH - 1) as b:
                attend(b, False)
            attend(BATCH - 1, True)

        @block.scalar
        def _(act):
            act.dma_start(lora_sb[:], lora_d[:, :]).then_inc(lora_in, 16)
            act.dma_start(w_sb[:, W_PF:], w_d[:, W_PF:]).then_inc(w_in, 16)
            act.sem_inc(exp_done, SLOTS)

            act.wait_ge(wfc_in, 16)
            nc.scalar.activation(abs_junk[:], w_sb[:, W_FC:W_FC + H], ACT.Abs, accum_out=wabs[:, 0:1]).then_inc(wabs_done, 1)
            act.wait_ge(w_in, 16)
            act.wait_ge(wabs_done, 1)
            nc.scalar.activation(abs_junk[:], w_sb[:, W_PF:W_PF + H], ACT.Abs, accum_out=wabs[:, 1:2]).then_inc(wabs_done, 1)

            def ln_norm(g, u):
                act.wait_ge(ln_nb_done, g // 2 + 1)
                wait(act, gram_done, g - 1)
                for t in range(2):
                    n = GT * g + t
                    nc.scalar.activation(xn_ring[:, u, t, 0:C], x_sb[:, n, :], ACT.Identity,
                                         bias=ln_nb[:, n:n + 1], scale=ln_r[:, n:n + 1]).then_inc(xn_act, 1)

            def x_hi(g, u):
                act.wait_ge(xT_done, g + 1)
                nc.scalar.activation(xT_hi[:, tokens(GT * g, GT)], banks[:, 5 + u, :], ACT.Copy).then_inc(xhi_done, 1)

            ln_norm(0, 0)
            for g in range(1, NG):
                ln_norm(g, g % 2)
                x_hi(g - 1, (g - 1) % 2)
                if g == 4:
                    act.wait_ge(prep_mm, 3)
                    nc.scalar.activation(wmT[:], banks[:, 0, 0:3 * C], ACT.Copy).then_inc(prep_wm, 1)
                    nc.scalar.activation(wm[:].rearrange("p j c -> p (j c)"), banks[:, 1, 0:3 * C], ACT.Copy).then_inc(prep_wm, 1)
                    nc.scalar.activation(woT[:], banks[:, 2, 0:C], ACT.Copy).then_inc(woT_done, 1)
            x_hi(NG - 1, 1)
            act.wait_ge(two_mm, 1)
            nc.scalar.activation(two_proj[:], banks[:, 4, 0:C], ACT.Copy).then_inc(two_done, 1)

            def gelus(g, u):
                for t in range(GT):
                    n = GT * g + t
                    act.wait_ge(h_done, n + 1)
                    if t == 0:
                        wait(act, zT_done, HC * (g - 1))
                    nc.scalar.activation(g_ring[:, u, t, :], banks[:, t % 2, :], ACT.Gelu,
                                         scale=1.0 / XS).then_inc(gelu_done, 1)

            def z_high(g, u):
                for c in range(HC):
                    act.wait_ge(zT_done, HC * g + c + 1)
                    if c == 0:
                        wait(act, f_done, g - 1)
                        act.wait_ge(lnw_done, 1)
                    nc.scalar.activation(z_hi[:, u, c, :], banks[:, 2 + c % 2, :], ACT.Copy,
                                         scale=lnw_s[:, c:c + 1]).then_inc(zhi_done, 1)

            def z_norm(g, u):
                act.wait_ge(fr_done, 2 * g + 2)
                nc.scalar.activation(g_ring[:, u, 3, :], g_ring[:, u, 3, :], ACT.Identity, bias=f_r[:, u, 1, 3:4],
                                     scale=f_r[:, u, 0, 3:4]).then_inc(z_act, 1)

            def f_scaled(g, u):
                act.wait_ge(f_done, g + 1)
                wait(act, fadd_done, g - 1)
                nc.scalar.activation(f_out[:, u, :], banks[:, 4, :], ACT.Copy, scale=ffn_scale[:, 0:1]).then_inc(fout_done, 1)

            gelus(0, 0)
            z_norm(0, 0)
            gelus(1, 1)
            z_high(0, 0)
            z_norm(1, 1)
            gelus(2, 0)
            z_high(1, 1)
            z_norm(2, 0)
            act.wait_ge(m_mm, 1)
            for t in range(GT):
                nc.scalar.activation(bias4[:, t, :], banks[:, 7, 257:257 + C], ACT.Copy).then_inc(bias_done, 1)
            f_scaled(0, 0)

            def ffn_step(g, u):
                gelus(g, u)
                z_high(g - 1, 1 - u)
                z_norm(g, u)
                f_scaled(g - 2, u)

            with act.Fori(1, 3) as p:
                ffn_step(2 * p + 1, 1)
                ffn_step(2 * p + 2, 0)
            ffn_step(7, 1)
            z_high(7, 1)
            f_scaled(6, 0)
            f_scaled(7, 1)

            act.wait_ge(m_split, 1)
            with act.Fori(0, NG // 2) as p:
                for u in range(2):
                    g = 2 * p + u
                    act.wait_ge(q_mm, g + 1)
                    nc.scalar.activation(qT_hi[:, tokens(GT * g, GT)], banks[:, 5 + 2 * u, :], ACT.Identity,
                                         bias=amax[:, 9:10]).then_inc(qhi_done, 1)
                    act.wait_ge(u_mm, g + 1)
                    nc.scalar.activation(u_hi[:, bass.ds(GT * g, GT), :], banks[:, 6 - 6 * u, :], ACT.Copy).then_inc(uhi_done, 1)

            def exps(b, k):
                n, par, slot, width = QT * b + k, k % 2, k % 4, P * (ORDER[k] + 1)
                act.wait_ge(nb_done, n + 1)
                transposed = CHUNK0[k - 1] if k else -CHUNKS[QT - 1]
                wait(act, eT_done, BATCH_CHUNKS * b + transposed + SLOTS)
                nc.scalar.activation(e_ring[:, par, 0:width],
                                     banks[:, 2 * par:2 * par + 2, :].rearrange("p a n -> p (a n)")[:, 0:width],
                                     ACT.Exp, bias=nbias[:, par:par + 1], scale=amax[:, 8:9],
                                     accum_out=rowsum[:, slot:slot + 1]).then_inc(exp_done, 1)

            def e_high(b, k):
                n, par, blocks = QT * b + k, k % 2, ORDER[k] + 1
                act.wait_ge(pv_done, n - 1 + SLOTS)
                for c in range(CHUNKS[k]):
                    j0, j1 = GT * c, min(GT * (c + 1), blocks)
                    act.wait_ge(eT_done, BATCH_CHUNKS * b + CHUNK0[k] + c + 1 + SLOTS)
                    nc.scalar.activation(eT_hi[:, par, j0:j1, :], banks[:, 5 + (CHUNK0[k] + c) % 2, 0:P * (j1 - j0)],
                                         ACT.Copy, scale=ES).then_inc(ehi_done, 1)

            exps(0, 0)
            exps(0, 1)
            e_high(0, 0)

            def attend(b, last):
                for k in range(QT):
                    if k + 1 < QT:
                        e_high(b, k + 1)
                    elif not last:
                        e_high(b + 1, 0)
                    if k + 2 < QT:
                        exps(b, k + 2)
                    elif not last:
                        exps(b + 1, k + 2 - QT)

            with act.Fori(0, BATCH - 1) as b:
                attend(b, False)
            attend(BATCH - 1, True)

        @block.vector
        def _(dve):
            seq = Sequence(dve, dve_seq)
            dve.sem_inc(qlo_done, SLOTS)
            dve.sem_inc(ulo_done, SLOTS)
            dve.sem_inc(fin_done, SLOTS)
            dve.sem_inc(elo_done, SLOTS)

            def ln_stats(p, step):
                for n in (8 * p + 2 * step, 8 * p + 2 * step + 1):
                    nc.vector.bn_stats(ln_st[:, n, :], x_sb[:, n, :]).then_inc(ln_stats_done, 1)

            def ln_moments(p, step):
                eight = slice(8 * p, 8 * p + 8)
                diff, total, mean2 = ln_tmp[:, 0, eight], ln_tmp[:, 1, eight], ln_tmp[:, 2, eight]
                if step == 0:
                    dve.wait_ge(ln_stats_done, 8 * (p + 1))
                    seq.mark(nc.vector.tensor_tensor(diff, ln_st[:, eight, 1], ln_st[:, eight, 4], ALU.subtract))
                    seq.mark(nc.vector.tensor_tensor(total, ln_st[:, eight, 2], ln_st[:, eight, 5], ALU.add))
                    seq.mark(nc.vector.tensor_tensor(mean2, ln_st[:, eight, 1], ln_st[:, eight, 4], ALU.add))
                if step == 1:
                    seq.settle()
                    seq.mark(nc.vector.tensor_tensor(diff, diff, diff, ALU.mult))
                    nc.vector.tensor_scalar(ln_nmean[:, eight], mean2, -0.5, None, ALU.mult).then_inc(ln_nmean_done, 1)
                if step == 2:
                    seq.settle()
                    seq.mark(nc.vector.scalar_tensor_tensor(total, diff, C / 4.0, total, ALU.mult, ALU.add))
                if step == 3:
                    seq.settle()
                    nc.vector.tensor_scalar(ln_arg[:, eight], total, 1.0 / (C * XS * XS), LN_EPS / (XS * XS),
                                            ALU.mult, ALU.add).then_inc(ln_arg_done, 1)

            def x_low(g):
                dve.wait_ge(xhi_done, g + 1)
                nc.vector.tensor_tensor(xT_lo[:, tokens(GT * g, GT)], banks[:, 5 + g % 2, :],
                                        xT_hi[:, tokens(GT * g, GT)], ALU.subtract).then_inc(xlo_done, 1)

            def threshold(k):
                dve.wait_ge(thr_sum, k + 1)
                seq.link(nc.vector.tensor_scalar(thr[:, 2 * k:2 * k + 1], banks[:, 4 - k, 0:1], 0.5 / (H * C), 0.5 * Q_EPS,
                                                 ALU.mult, ALU.add))
                seq.link(nc.vector.tensor_scalar(thr[:, 2 * k + 1:2 * k + 2], thr[:, 2 * k:2 * k + 1], -1.0, None, ALU.mult))

            def quantise(k, src, dst):
                seq.link(nc.vector.tensor_scalar(below[:], src, thr[:, 2 * k + 1:2 * k + 2], None, ALU.is_lt))
                return nc.vector.scalar_tensor_tensor(dst, src, thr[:, 2 * k:2 * k + 1], below[:], ALU.is_gt, ALU.subtract)

            for p in range(4):
                dve.wait_ge(x_in[p], 16)
                for step in range(4):
                    ln_stats(p, step)
                    if p > 1:
                        ln_moments(p - 1, step)
                if p == 0:
                    for step in range(4):
                        ln_moments(0, step)
                if p == 1:
                    threshold(0)
                    quantise(0, w_sb[:, W_FC:W_FC + H], wq_fc[:]).then_inc(wq_fc_done, 1)
                    dve.wait_ge(w_in, 16)
                    nc.vector.tensor_reduce(lnw_abs[:, 0:1], lnw_c, axis=AXX, op=ALU.max,
                                            apply_absolute_value=True).then_inc(lnw_red, 1)
                if p >= 2:
                    x_low(2 * p - 4)
                    x_low(2 * p - 3)
            for step in range(4):
                ln_moments(3, step)
            threshold(1)
            seq.mark(quantise(1, w_sb[:, W_PF:W_PF + H], wq_pf32[:].rearrange("p k c -> p (k c)")))
            x_low(4)
            seq.settle()
            nc.vector.tensor_copy(wq_pf[:], wq_pf32[:]).then_inc(wq_pf_done, 1)
            dve.wait_ge(lnw_all, 1)
            seq.link(nc.vector.tensor_scalar(ffn_scale[:, 0:1], lnw_abs[:, 1:2], 1.0 / ZS, 1e-30, ALU.mult, ALU.max))
            seq.mark(nc.vector.reciprocal(ffn_scale[:, 1:2], ffn_scale[:, 0:1]))
            x_low(5)
            seq.settle()
            nc.vector.tensor_scalar(lnw_s[:], lnw_c, ffn_scale[:, 1:2], None, ALU.mult).then_inc(lnw_done, 1)
            seq.mark(nc.vector.tensor_copy(lnb_bc[:], lnb_c.unsqueeze(2).broadcast_to([P, HC, P])))
            x_low(6)
            x_low(7)
            dve.wait_ge(gram_done, NG)
            nc.vector.tensor_copy(gram[:], banks[:, 7, 0:C + 1]).then_inc(gram_cp, 1)

            def f_stats(g, u):
                def stats(t):
                    dve.wait_ge(gelu_done, GT * g + t + 1)
                    seq.mark(nc.vector.bn_stats(fst[:, u, t, :], g_ring[:, u, t, :]))

                def aggregate(half):
                    for t in (2 * half, 2 * half + 1):
                        seq.mark(nc.vector.bn_aggr(f_mv[:, u, t, :], fst[:, u, t, :]))

                def arguments(half):
                    two = slice(2 * half, 2 * half + 2)
                    nc.vector.tensor_scalar(f_arg[:, u, 1, two], f_mv[:, u, two, 0], -1.0, None, ALU.mult)\
                        .then_inc(fneg_done, 1)
                    nc.vector.tensor_scalar(f_arg[:, u, 0, two], f_mv[:, u, two, 1], LN_EPS, None, ALU.add)\
                        .then_inc(farg_done, 1)

                stats(0)
                stats(1)
                stats(2)
                seq.settle()
                stats(3)
                aggregate(0)
                seq.settle()
                arguments(0)
                aggregate(1)
                seq.settle()
                arguments(1)

            F_STATS = 2 * GT

            def z_low(g, u):
                wait(dve, f_done, g - 1)
                for c in range(HC):
                    dve.wait_ge(zhi_done, HC * g + c + 1)
                    nc.vector.scalar_tensor_tensor(z_lo[:, u, c, :], banks[:, 2 + c % 2, :], lnw_s[:, c:c + 1],
                                                   z_hi[:, u, c, :], ALU.mult, ALU.subtract).then_inc(zlo_done, 1)

            f_stats(0, 0)
            dve.wait_ge(bn_z, 1)
            zb = banks[:, 5, 0:3 * (C + 1)].rearrange("p (j c) -> p j c", j=3)
            for j in range(3):
                seq.link(nc.vector.tensor_tensor_reduce(out=bn_prod[:], in0=zb[:, j, 0:C], in1=wm[:, j, :], scale=1.0, scalar=0.0,
                                                        op0=ALU.mult, op1=ALU.add, accum_out=bn[:, 0, j:j + 1]))
            seq.link(nc.vector.tensor_scalar(bn[:, 1, :], zb[:, :, C], 1.0 / (XS * TOKENS), None, ALU.mult))
            seq.link(nc.vector.tensor_tensor(bn[:, 2, :], bn[:, 1, :], bn[:, 1, :], ALU.mult))
            seq.link(nc.vector.scalar_tensor_tensor(bn[:, 3, :], bn[:, 0, :], 1.0 / (XS * XS * TOKENS), bn[:, 2, :],
                                                    ALU.mult, ALU.subtract))
            nc.vector.tensor_scalar(bn[:, 4, :], bn[:, 3, :], 0.0, BN_EPS, ALU.max, ALU.add).then_inc(bn_arg, 1)
            f_stats(1, 1)
            dve.wait_ge(bn_pow, 1)
            seq.link(nc.vector.tensor_tensor(bn[:, 6, :], gamma_c, bn[:, 5, :], ALU.mult))
            seq.link(nc.vector.tensor_tensor(bn[:, 7, :], bn[:, 1, :], bn[:, 6, :], ALU.mult))
            seq.link(nc.vector.tensor_tensor(bn[:, 8, :], beta_c, bn[:, 7, :], ALU.subtract))
            seq.mark(nc.vector.tensor_tensor(bn[:, 9, 0:1], bn[:, 6, 0:1], bn[:, 6, 1:2], ALU.mult))
            nc.vector.tensor_tensor(bn[:, 10, 0:1], bn[:, 8, 0:1], bn[:, 6, 1:2], ALU.mult).then_inc(bn_w, 1)
            nc.vector.tensor_scalar(wv_scaled[:], wm[:, 2, :], bn[:, 6, 2:3], None, ALU.mult).then_inc(bn_w, 1)
            nc.vector.tensor_copy(bv_bc[:], bn[:, 8, 2:3].broadcast_to([P, P])).then_inc(bn_w, 1)
            seq.settle()
            nc.vector.tensor_scalar(wq_scaled[:], wm[:, 0, :], bn[:, 9, 0:1], None, ALU.mult).then_inc(bn_w, 1)
            z_low(0, 0)
            dve.wait_ge(m_mm, 1)
            seq.mark(nc.vector.tensor_copy(m_f[:], banks[:, 7, 0:C + 1]))
            seq.mark(nc.vector.tensor_copy(u_f[:], banks[:, 7, C + 1:2 * C + 1]))
            seq.settle()
            seq.mark(nc.vector.tensor_reduce(amax[:, 0:1], m_f[:], axis=AXX, op=ALU.max, apply_absolute_value=True))
            seq.mark(nc.vector.tensor_reduce(amax[:, 1:2], u_f[:], axis=AXX, op=ALU.max, apply_absolute_value=True))
            seq.settle()
            nc.vector.tensor_copy(amax[:, 0:2], amax[:, 0:2]).then_inc(m_abs, 1)
            f_stats(2, 0)
            z_low(1, 1)
            dve.wait_ge(m_all, 1)
            seq.mark(nc.vector.tensor_scalar(amax[:, 4:5], amax[:, 2:3], 1.0, 1.0 / MS, ALU.max, ALU.mult))
            seq.mark(nc.vector.tensor_scalar(amax[:, 5:6], amax[:, 3:4], 1e-30, 1.0 / MS, ALU.max, ALU.mult))
            seq.settle()
            seq.mark(nc.vector.reciprocal(amax[:, 6:8], amax[:, 4:6]))
            seq.mark(nc.vector.tensor_scalar(amax[:, 8:9], amax[:, 4:5], float(C) ** -0.5 / (XS * XS), None, ALU.mult))
            seq.settle()
            seq.mark(nc.vector.tensor_scalar(m_f[:], m_f[:], amax[:, 6:7], None, ALU.mult))
            seq.mark(nc.vector.tensor_scalar(u_f[:], u_f[:], amax[:, 7:8], None, ALU.mult))
            seq.settle()
            seq.mark(nc.vector.tensor_copy(m_hi[:], m_f[:, 0:C]))
            seq.mark(nc.vector.tensor_copy(u_hi_w[:], u_f[:]))
            seq.mark(nc.vector.tensor_scalar(amax[:, 9:10], m_f[:, C:C + 1], XS, None, ALU.mult))
            seq.settle()
            seq.mark(nc.vector.tensor_scalar(amax[:, 7:8], amax[:, 7:8], XS * ES, None, ALU.mult))
            seq.link(nc.vector.tensor_tensor(m_lo[:], m_f[:, 0:C], m_hi[:], ALU.subtract))
            nc.vector.tensor_tensor(u_lo_w[:], u_f[:], u_hi_w[:], ALU.subtract).then_inc(m_split, 1)

            start = seq.count
            with dve.Fori(1, 3) as p:
                seq.count = start + 2 * F_STATS * (p - 1)
                f_stats(2 * p + 1, 1)
                z_low(2 * p, 0)
                f_stats(2 * p + 2, 0)
                z_low(2 * p + 1, 1)
            seq.count = start + 4 * F_STATS
            f_stats(7, 1)
            z_low(6, 0)
            z_low(7, 1)

            with dve.Fori(0, NG // 2) as p:
                for u in range(2):
                    g = 2 * p + u
                    dve.wait_ge(qhi_done, g + 1)
                    nc.vector.scalar_tensor_tensor(qT_lo[:, tokens(GT * g, GT)], banks[:, 5 + 2 * u, :], amax[:, 9:10],
                                                   qT_hi[:, tokens(GT * g, GT)], ALU.add, ALU.subtract).then_inc(qlo_done, 1)
                    dve.wait_ge(uhi_done, g + 1)
                    nc.vector.tensor_tensor(u_lo[:, bass.ds(GT * g, GT), :],
                                            banks[:, 6 - 6 * u, :].rearrange("p (t c) -> p t c", t=GT),
                                            u_hi[:, bass.ds(GT * g, GT), :], ALU.subtract).then_inc(ulo_done, 1)

            def row_max(b, k):
                n, par = QT * b + k, k % 2
                dve.wait_ge(s_done, n + 1)
                nc.vector.tensor_reduce(
                    nmax[:, par:par + 1],
                    banks[:, 2 * par:2 * par + 2, :].rearrange("p a n -> p (a n)")[:, 0:P * (ORDER[k] + 1)],
                    axis=AXX, op=ALU.max, negate=True).then_inc(max_done, 1)

            def e_low(b, k):
                n, par = QT * b + k, k % 2
                dve.wait_ge(pv_done, n - 1 + SLOTS)
                for c in range(CHUNKS[k]):
                    j0, j1 = GT * c, min(GT * (c + 1), ORDER[k] + 1)
                    dve.wait_ge(ehi_done, BATCH_CHUNKS * b + CHUNK0[k] + c + 1)
                    nc.vector.scalar_tensor_tensor(eT_lo[:, par, j0:j1, :].rearrange("p j t -> p (j t)"),
                                                   banks[:, 5 + (CHUNK0[k] + c) % 2, 0:P * (j1 - j0)], ES,
                                                   eT_hi[:, par, j0:j1, :].rearrange("p j t -> p (j t)"),
                                                   ALU.mult, ALU.subtract).then_inc(elo_done, 1)

            def row_inverse(b, k):
                n, slot = QT * b + k, k % 4
                dve.wait_ge(sum_done, n + 1)
                seq.mark(nc.vector.reciprocal(rinv[:, slot:slot + 1], rowsum_s[:, slot:slot + 1]))

            def finish(b, k):
                n, slot = QT * b + k, k % 4
                seq.settle()
                dve.wait_ge(pv_done, n + 1 + SLOTS)
                dve.wait_ge(badd_done, NG)
                row = x_sb[:, bass.ds(QT * b + ORDER[k], 1), :].rearrange("p o c -> p (o c)")
                nc.vector.scalar_tensor_tensor(row, banks[:, 4 + 3 * (k % 2), 0:C], rinv[:, slot:slot + 1], row,
                                               ALU.mult, ALU.add).then_inc(fin_done, 1)

            row_max(0, 0)
            row_max(0, 1)
            e_low(0, 0)

            def attend(b, last):
                for k in range(QT):
                    row_inverse(b, k)
                    if k + 2 < QT:
                        row_max(b, k + 2)
                    elif not last:
                        row_max(b + 1, k + 2 - QT)
                    if k + 1 < QT:
                        e_low(b, k + 1)
                    elif not last:
                        e_low(b + 1, 0)
                    finish(b, k)

            start = seq.count
            with dve.Fori(0, BATCH - 1) as b:
                seq.count = start + QT * b
                attend(b, False)
            seq.count = start + QT * (BATCH - 1)
            attend(BATCH - 1, True)

        @block.tensor
        def _(pe):
            mm = nc.tensor.matmul
            pe.sem_inc(eT_done, SLOTS)
            pe.sem_inc(pv_done, SLOTS)
            pe.wait_ge(consts, 1)
            pe.wait_ge(wabs_done, 1)
            mm(banks[:, 4, 0:1], ones[:], wabs[:, 0:1], start=True, stop=True).then_inc(thr_sum, 1)

            def ln_products(g, u, first):
                pe.wait_ge(xn_act, 2 * (g + 1))
                pe.wait_ge(xn_pool, 2 * (g + 1))
                wait(pe, xlo_done, g - 1)
                for t in range(GT):
                    last = nc.tensor.transpose(banks[:, 5 + u, tokens(t)], xn_ring[:, u, t, 0:C], ident[:])
                last.then_inc(xT_done, 1)
                for t in range(GT):
                    last = mm(banks[:, 7, 0:C + 1], xn_ring[:, u, t, 0:C], xn_ring[:, u, t, :], start=(first and t == 0),
                              stop=(isinstance(g, int) and g == NG - 1 and t == GT - 1))
                last.then_inc(gram_done, 1)

            pe.wait_ge(w_in, 16)
            pe.wait_ge(consts, 8)
            pe.wait_ge(lora_in, 16)
            for m in range(3):
                mm(banks[:, 0, 0:3 * C], lora_sb[:, L_B + C * m:L_B + C * (m + 1)], az[:, m, :], start=(m == 0), stop=False)
            mm(banks[:, 0, 0:3 * C], ident[:], w_sb[:, W_QKVT:W_QKVT + 3 * C], start=False, stop=True).then_inc(prep_mm, 1)
            for j in range(3):
                to = banks[:, 1, C * j:C * (j + 1)]
                for m in range(3):
                    mm(to, az[:, m, C * j:C * (j + 1)], lora_sb[:, L_B + C * m:L_B + C * (m + 1)], start=(m == 0), stop=False)
                last = mm(to, ident[:], w_sb[:, W_QKV + C * j:W_QKV + C * (j + 1)], start=False, stop=True)
            last.then_inc(prep_mm, 1)
            mm(banks[:, 2, 0:C], lora_sb[:, L_PB:L_PB + C], lora_sb[:, L_PAT:L_PAT + C], start=True, stop=False)
            mm(banks[:, 2, 0:C], ident[:], w_sb[:, W_OT:W_OT + C], start=False, stop=True).then_inc(prep_mm, 1)
            pe.wait_ge(wabs_done, 2)
            mm(banks[:, 3, 0:1], ones[:], wabs[:, 1:2], start=True, stop=True).then_inc(thr_sum, 1)
            for g in range(NG):
                ln_products(g, g % 2, g == 0)
            pe.wait_ge(woT_done, 1)
            pe.wait_ge(wq_fc_done, 1)
            mm(banks[:, 4, 0:C], w_sb[:, W_O:W_O + C], woT[:], start=True, stop=True).then_inc(two_mm, 1)
            pe.wait_ge(wq_fc_done, 1)

            def ffn_up(g):
                for t in range(GT):
                    n = GT * g + t
                    wait(pe, gelu_done, n - 1)
                    mm(banks[:, t % 2, :], xT_hi[:, tokens(n)], wq_fc[:], start=True, stop=False)
                    mm(banks[:, t % 2, :], xT_lo[:, tokens(n)], wq_fc[:], start=False, stop=True).then_inc(h_done, 1)

            def z_transposes(g, u, chunks):
                for c in chunks:
                    if c == 0:
                        pe.wait_ge(z_pool, 3 * (g + 1))
                        pe.wait_ge(z_act, g + 1)
                    wait(pe, zlo_done, HC * g + c - 1)
                    for t in range(GT):
                        last = nc.tensor.transpose(banks[:, 2 + c % 2, tokens(t)], g_ring[:, u, t, tokens(c)], ident[:])
                    last.then_inc(zT_done, 1)

            def ffn_down(g, u, tiles):
                for t in tiles:
                    if t == 0:
                        pe.wait_ge(zlo_done, HC * (g + 1))
                        wait(pe, fout_done, g)
                    for c in range(HC):
                        mm(banks[:, 4, tokens(t)], z_hi[:, u, c, tokens(t)], wq_pf[:, c, :], start=(c == 0), stop=False)
                        last = mm(banks[:, 4, tokens(t)], z_lo[:, u, c, tokens(t)], wq_pf[:, c, :],
                                  start=False, stop=(c == HC - 1))
                    if t == GT - 1:
                        last.then_inc(f_done, 1)

            def ffn_step(g, u):
                ffn_up(g)
                z_transposes(g - 1, 1 - u, (0, 1))
                ffn_down(g - 2, u, (0, 1))
                z_transposes(g - 1, 1 - u, (2,))
                ffn_down(g - 2, u, (2,))
                z_transposes(g - 1, 1 - u, (3,))
                ffn_down(g - 2, u, (3,))

            pe.wait_ge(xlo_done, NG)
            pe.wait_ge(prep_wm, 2)
            ffn_up(0)
            pe.wait_ge(gram_cp, 1)
            for j in range(3):
                last = mm(banks[:, 5, (C + 1) * j:(C + 1) * (j + 1)], wmT[:, C * j:C * (j + 1)], gram[:], start=True, stop=True)
            last.then_inc(bn_z, 1)
            ffn_up(1)
            pe.wait_ge(two_done, 1)
            pe.wait_ge(wq_pf_done, 1)
            z_transposes(0, 0, range(HC))
            pe.wait_ge(bn_w, 4)
            mm(banks[:, 7, 0:C], wq_scaled[:], wm[:, 1, :], start=True, stop=True)
            mm(banks[:, 7, C:C + 1], wm[:, 1, :], bn[:, 10, 0:1], start=True, stop=True)
            mm(banks[:, 7, C + 1:2 * C + 1], wv_scaled[:], two_proj[:], start=True, stop=True)
            mm(banks[:, 7, 257:257 + C], bv_bc[:], two_proj[:], start=True, stop=False)
            for c in range(HC):
                last = mm(banks[:, 7, 257:257 + C], lnb_bc[:, c, :], wq_pf32[:, c, :], start=False, stop=(c == HC - 1))
            last.then_inc(m_mm, 1)
            ffn_step(2, 0)
            with pe.Fori(1, 3) as p:
                ffn_step(2 * p + 1, 1)
                ffn_step(2 * p + 2, 0)
            ffn_step(7, 1)
            z_transposes(7, 1, (0, 1))
            ffn_down(6, 0, range(GT))
            z_transposes(7, 1, (2, 3))
            ffn_down(7, 1, range(GT))

            pe.wait_ge(m_split, 1)
            pe.wait_ge(bias_done, GT)
            with pe.Fori(0, NG // 2) as p:
                for u in range(2):
                    g = 2 * p + u
                    xs = tokens(GT * g, GT)
                    q_bank = banks[:, 5 + 2 * u, :]
                    pe.wait_ge(qlo_done, g - 1 + SLOTS)
                    pe.wait_ge(ulo_done, g - 1 + SLOTS)
                    mm(q_bank, m_hi[:], xT_hi[:, xs], start=True, stop=False)
                    mm(q_bank, m_hi[:], xT_lo[:, xs], start=False, stop=False)
                    mm(q_bank, m_lo[:], xT_hi[:, xs], start=False, stop=True).then_inc(q_mm, 1)
                    for t in range(GT):
                        n, to = GT * g + t, banks[:, 6 - 6 * u, tokens(t)]
                        mm(to, xT_hi[:, tokens(n)], u_hi_w[:], start=True, stop=False)
                        mm(to, xT_hi[:, tokens(n)], u_lo_w[:], start=False, stop=False)
                        last = mm(to, xT_lo[:, tokens(n)], u_hi_w[:], start=False, stop=True)
                    last.then_inc(u_mm, 1)
            pe.wait_ge(qlo_done, NG + SLOTS)
            pe.wait_ge(ulo_done, NG + SLOTS)

            def scores(b, k):
                n, par, width = QT * b + k, k % 2, P * (ORDER[k] + 1)
                pe.wait_ge(exp_done, n - 1 + SLOTS)
                for c in range(CHUNKS[k]):
                    lo, hi = 512 * c, min(512 * (c + 1), width)
                    to, keys = banks[:, 2 * par + c, 0:hi - lo], bass.ds(T * b + lo, hi - lo)
                    query = tokens(QT * b + ORDER[k])
                    diagonal = c == CHUNKS[k] - 1
                    mm(to, qT_hi[:, query], xT_hi[:, keys], start=True, stop=False)
                    mm(to, qT_hi[:, query], xT_lo[:, keys], start=False, stop=False)
                    last = mm(to, qT_lo[:, query], xT_hi[:, keys], start=False, stop=not diagonal)
                    if diagonal:
                        last = mm(banks[:, 2 * par + c, hi - lo - P:hi - lo], ident_bf[:], mask_bf[:], start=False, stop=True)
                last.then_inc(s_done, 1)

            def transpose_probs(b, k):
                n, par = QT * b + k, k % 2
                pe.wait_ge(exp_done, n + 1 + SLOTS)
                for c in range(CHUNKS[k]):
                    chunk = CHUNK0[k] + c
                    pe.wait_ge(elo_done, BATCH_CHUNKS * b + chunk - 1 + SLOTS)
                    for j in range(GT * c, min(GT * (c + 1), ORDER[k] + 1)):
                        last = nc.tensor.transpose(banks[:, 5 + chunk % 2, tokens(j - GT * c)], e_ring[:, par, tokens(j)],
                                                   ident[:])
                    last.then_inc(eT_done, 1)

            def attend_values(b, k):
                n, par, blocks = QT * b + k, k % 2, ORDER[k] + 1
                pe.wait_ge(elo_done, BATCH_CHUNKS * b + CHUNK0[k] + CHUNKS[k] + SLOTS)
                pe.wait_ge(fin_done, n - 1 + SLOTS)
                to = banks[:, 4 + 3 * par, 0:C]
                for j in range(blocks):
                    vh = u_hi[:, bass.ds(QT * b + j, 1), :].rearrange("p o c -> p (o c)")
                    vl = u_lo[:, bass.ds(QT * b + j, 1), :].rearrange("p o c -> p (o c)")
                    mm(to, eT_hi[:, par, j, :], vh, start=(j == 0), stop=False)
                    mm(to, eT_hi[:, par, j, :], vl, start=False, stop=False)
                    last = mm(to, eT_lo[:, par, j, :], vh, start=False, stop=(j == blocks - 1))
                last.then_inc(pv_done, 1)

            scores(0, 0)
            scores(0, 1)
            transpose_probs(0, 0)

            def attend(b, last):
                for k in range(QT):
                    if k + 2 < QT:
                        scores(b, k + 2)
                    elif not last:
                        scores(b + 1, k + 2 - QT)
                    if k + 1 < QT:
                        transpose_probs(b, k + 1)
                    elif not last:
                        transpose_probs(b + 1, 0)
                    attend_values(b, k)

            with pe.Fori(0, BATCH - 1) as b:
                attend(b, False)
            attend(BATCH - 1, True)


def kernel(L0_attn_x, L0_attn_W_attn, L0_attn_W_proj, L0_attn_lora_attn_A, L0_attn_lora_attn_B, L0_attn_lora_proj_A,
           L0_attn_lora_proj_B, L0_attn_bn_gamma, L0_attn_bn_beta, L0_ffn_W_fc, L0_ffn_ln_w, L0_ffn_ln_b, L0_ffn_W_proj):
    import numpy as np
    import concourse.bacc as bacc
    from concourse.bass_utils import run_bass_kernel_spmd

    def rows_to_partitions(a):
        return a.reshape(-1, P, a.shape[-1]).transpose(1, 0, 2).reshape(P, -1)

    a = {k: np.asarray(v) for k, v in dict(
        x=L0_attn_x, wa=L0_attn_W_attn, wo=L0_attn_W_proj, aA=L0_attn_lora_attn_A, aB=L0_attn_lora_attn_B,
        pA=L0_attn_lora_proj_A, pB=L0_attn_lora_proj_B, gamma=L0_attn_bn_gamma, beta=L0_attn_bn_beta, fc=L0_ffn_W_fc,
        lw=L0_ffn_ln_w, lb=L0_ffn_ln_b, pf=L0_ffn_W_proj).items()}
    weights = np.concatenate([
        a["fc"].T, rows_to_partitions(a["pf"].T), rows_to_partitions(a["wa"]), a["wa"].T, a["wo"], a["wo"].T,
        a["lw"].reshape(HC, P).T, a["lb"].reshape(HC, P).T, a["gamma"].reshape(3, P).T, a["beta"].reshape(3, P).T], axis=1)
    lora = np.concatenate([a["aA"].T, a["aB"], a["pA"].T, a["pB"]], axis=1)

    nc = bacc.Bacc("TRN2", target_bir_lowering=False, num_devices=1)
    arrays = {"x_dram": np.ascontiguousarray(a["x"]), "w_dram": np.ascontiguousarray(weights),
              "lora_dram": np.ascontiguousarray(lora)}
    ins = [nc.dram_tensor(n, v.shape, mybir.dt.from_np(v.dtype), kind="ExternalInput").ap() for n, v in arrays.items()]
    out = nc.dram_tensor("out_dram", a["x"].shape, F32, kind="ExternalOutput").ap()
    block_kernel(nc, *ins, out)
    r = run_bass_kernel_spmd(nc, [arrays], core_ids=[0])
    return r.results[0]["out_dram"]
```

```python
from contextlib import ExitStack

import concourse.bass as bass
from concourse import mybir

F32, F16, BF16 = mybir.dt.float32, mybir.dt.float16, mybir.dt.bfloat16
ALU = mybir.AluOpType
ACT = mybir.ActivationFunctionType
AXX = mybir.AxisListType.X
REDUCE_ABSMAX = bass.bass_isa.ReduceOp.absmax

P = 128
BATCH, T, C, R, H = 4, 1024, 128, 64, 512
TOKENS = BATCH * T
NT = TOKENS // P
GT = 4
NG = NT // GT
QT = T // P
HC = H // P
LN_EPS, BN_EPS, Q_EPS = 1e-5, 1e-5, 1e-6

XS = 16.0
MS = 16.0
ZS = 64.0
ES = 4096.0
SLOTS = 2
MASKED = -float(2 ** 36)

ORDER = [0, 2, 4, 6, 7, 5, 3, 1]
CHUNKS = [1 if i < GT else 2 for i in ORDER]
CHUNK0 = [sum(CHUNKS[:k]) for k in range(QT)]
BATCH_CHUNKS = sum(CHUNKS)

LN_BLOCKS = [(0, 4), (4, 8), (8, 12), (12, 16), (16, 24), (24, 32)]
LN_BLOCK_OF = [next(i for i, (a, b) in enumerate(LN_BLOCKS) if a <= GT * g < b) for g in range(NG)]
ACT_TILES = [3, 3, 3, 3, 3, 2, 2, 2]
XN_SLOTS = 4
XT_BANKS = [5, 6]
ZT_BANKS = [2, 3, 5, 6]
QU_SLOTS = 3
Q_BANKS, U_BANKS = [3, 0, 1], [5, 7, 2]
WARM_UP = 10

W_FC, W_PF, W_QKV, W_QKVT, W_O, W_OT, W_COLS = 0, 512, 1024, 1408, 1792, 1920, 2048
N_COLS = 2 * HC + 6
L_AT, L_B, L_PAT, L_PB, L_END = 0, 128, 512, 640, 768


def block_kernel(nc, x_d, w_d, lora_d, out_d):
    x_v = x_d.rearrange("b (n p) c -> p (b n) c", p=P)
    out_v = out_d.rearrange("b (n p) c -> p (b n) c", p=P)
    with ExitStack() as ctx:
        def sb(name, shape, dt=F32):
            return ctx.enter_context(nc.sbuf_tensor(name, shape, dt))

        def sem(name):
            return ctx.enter_context(nc.semaphore(name))

        x_sb = sb("x_sb", [P, NT, C])
        w_sb = sb("w_sb", [P, W_COLS + N_COLS])
        lora_sb = sb("lora_sb", [R, L_END])
        ident = sb("ident", [P, P])
        ident_bf = sb("ident_bf", [P, P], BF16)
        mask_bf = sb("mask_bf", [P, P], BF16)
        ones = sb("ones", [P, P])
        az = sb("az", [R, 3, 3 * C])
        neg_half = sb("neg_half", [P, 2 * GT])
        xn_ring = sb("xn_ring", [P, XN_SLOTS, GT, C + 1])
        xT_hi = sb("xT_hi", [P, TOKENS], F16)
        xT_lo = sb("xT_lo", [P, TOKENS], F16)
        ln_st = sb("ln_st", [P, NT, 6])
        ln_mv = sb("ln_mv", [P, NT, 2])
        ln_nmean = sb("ln_nmean", [P, NT])
        ln_arg = sb("ln_arg", [P, NT])
        ln_r = sb("ln_r", [P, NT])
        ln_nb = sb("ln_nb", [P, NT])
        table_in = sb("table_in", [P, 1])
        table_out = sb("table_out", [P, 2])
        wabs = sb("wabs", [P, 2])
        thr = sb("thr", [P, 4])
        abs_junk = sb("abs_junk", [P, H])
        below = sb("below", [P, H], F16)
        wq_fc = sb("wq_fc", [P, H], F16)
        wq_pf = sb("wq_pf", [P, HC, C], F16)
        wq_pf32 = sb("wq_pf32", [P, HC, C])
        lnb_bc = sb("lnb_bc", [P, HC, P])
        lnw_abs = sb("lnw_abs", [P, 2])
        lnw_s = sb("lnw_s", [P, HC])
        ffn_scale = sb("ffn_scale", [P, 2])
        wm = sb("wm", [P, 3, C])
        wmT = sb("wmT", [P, 3 * C])
        woT = sb("woT", [P, C])
        two_proj = sb("two_proj", [P, C])
        gram = sb("gram", [P, C + 1])
        bn_prod = sb("bn_prod", [P, 3, C])
        bn = sb("bn", [P, 11, 3])
        wq_scaled = sb("wq_scaled", [P, C])
        wv_scaled = sb("wv_scaled", [P, C])
        bv_bc = sb("bv_bc", [P, P])
        amax = sb("amax", [P, 11])
        m_bias = sb("m_bias", [P, 1])
        m_hi = sb("m_hi", [P, C], F16)
        m_lo = sb("m_lo", [P, C], F16)
        u_hi_w = sb("u_hi_w", [P, C], F16)
        u_lo_w = sb("u_lo_w", [P, C], F16)
        bias4 = sb("bias4", [P, GT, C])
        g_ring = sb("g_ring", [P, 2, GT, H])
        fst = sb("fst", [P, 2, GT, 6])
        f_mv = sb("f_mv", [P, 2, GT, 2])
        f_arg = sb("f_arg", [P, 2, 2, GT])
        f_r = sb("f_r", [P, 2, 2, GT])
        f_out = sb("f_out", [P, 2, GT * C])
        z_hi = sb("z_hi", [P, 2, HC, GT * P], F16)
        z_lo = sb("z_lo", [P, 2, HC, GT * P], F16)
        qT_hi = sb("qT_hi", [P, TOKENS], F16)
        qT_lo = sb("qT_lo", [P, TOKENS], F16)
        u_hi = sb("u_hi", [P, NT, C], F16)
        u_lo = sb("u_lo", [P, NT, C], F16)
        e_ring = sb("e_ring", [P, 2, T])
        eT_hi = sb("eT_hi", [P, 2, QT, P], F16)
        eT_lo = sb("eT_lo", [P, 2, QT, P], F16)
        nmax = sb("nmax", [P, 2])
        nbias = sb("nbias", [P, 2])
        rowsum = sb("rowsum", [P, 4])
        rowsum_s = sb("rowsum_s", [P, 4])
        rinv = sb("rinv", [P, 4])

        banks = ctx.enter_context(nc.psum_tensor("banks", [P, 8, 512], F32))

        cols = w_sb[:, W_COLS:W_COLS + N_COLS]
        lnw_c, lnb_c = cols[:, 0:HC], cols[:, HC:2 * HC]
        gamma_c, beta_c = cols[:, 2 * HC:2 * HC + 3], cols[:, 2 * HC + 3:2 * HC + 6]

        x_in = [sem(f"x_in{k}") for k in range(len(LN_BLOCKS))]
        wfc_in, w_in, lora_in = sem("wfc_in"), sem("w_in"), sem("lora_in")
        consts = sem("consts")
        dve_seq = sem("dve_seq")
        pool_seq = sem("pool_seq")
        wabs_done, thr_sum, table_ready = sem("wabs_done"), sem("thr_sum"), sem("table_ready")
        wq_fc_done, wq_pf_done = sem("wq_fc_done"), sem("wq_pf_done")
        ln_nmean_done = sem("ln_nmean_done")
        ln_arg_done, ln_nb_done = sem("ln_arg_done"), sem("ln_nb_done")
        xn_act, xn_pool, xT_done, xhi_done, xlo_done, gram_done = (
            sem("xn_act"), sem("xn_pool"), sem("xT_done"), sem("xhi_done"), sem("xlo_done"), sem("gram_done"))
        prep_mm, prep_wm, woT_done, two_mm, two_done = (
            sem("prep_mm"), sem("prep_wm"), sem("woT_done"), sem("two_mm"), sem("two_done"))
        pf32_done, lnb_done = sem("pf32_done"), sem("lnb_done")
        lnw_red, lnw_all, lnw_done = sem("lnw_red"), sem("lnw_all"), sem("lnw_done")
        h_done, gelu_done, farg_done = sem("h_done"), sem("gelu_done"), sem("farg_done")
        fr_done, z_pool, z_act = sem("fr_done"), sem("z_pool"), sem("z_act")
        zT_done, zhi_done, zlo_done, f_done, fout_done, fadd_done = (
            sem("zT_done"), sem("zhi_done"), sem("zlo_done"), sem("f_done"), sem("fout_done"), sem("fadd_done"))
        gram_cp, bn_z, bn_sums, bn_w, m_mm = (
            sem("gram_cp"), sem("bn_z"), sem("bn_sums"), sem("bn_w"), sem("m_mm"))
        m_abs, m_all, m_scale, m_split, bias_done = (
            sem("m_abs"), sem("m_all"), sem("m_scale"), sem("m_split"), sem("bias_done"))
        q_mm, qhi_done, qlo_done = sem("q_mm"), sem("qhi_done"), sem("qlo_done")
        u_mm, uhi_done, ulo_done, badd_done = sem("u_mm"), sem("uhi_done"), sem("ulo_done"), sem("badd_done")
        max_done, sum_done = sem("max_done"), sem("sum_done")
        s_done, nb_done, exp_done, eT_done, ehi_done, elo_done, pv_done, fin_done = (
            sem("s_done"), sem("nb_done"), sem("exp_done"), sem("eT_done"), sem("ehi_done"),
            sem("elo_done"), sem("pv_done"), sem("fin_done"))
        out_done = sem("out_done")

        block = ctx.enter_context(nc.Block())

        def wait(eng, semaphore, value):
            if not isinstance(value, int) or value > 0:
                eng.wait_ge(semaphore, value)

        class Sequence:

            def __init__(self, eng, semaphore):
                self.eng, self.semaphore, self.count = eng, semaphore, 0

            def mark(self, instruction):
                instruction.then_inc(self.semaphore, 1)
                self.count = self.count + 1

            def settle(self, running=0):
                self.eng.wait_ge(self.semaphore, self.count - running)

            def link(self, instruction):
                self.mark(instruction)
                self.settle()

        def tokens(n, k=1):
            return bass.ds(n * P, k * P)

        @block.sync
        def _(sp):
            for k, (first, end) in enumerate(LN_BLOCKS):
                if k == 4:
                    sp.dma_start(w_sb[:, W_FC:W_PF], w_d[:, W_FC:W_PF]).then_inc(wfc_in, 16)
                sp.dma_start(x_sb[:, first:end, :], x_v[:, first:end, :]).then_inc(x_in[k], 16)
            sp.dma_start(w_sb[:, W_PF:], w_d[:, W_PF:]).then_inc(w_in, 16)
            with sp.Fori(0, BATCH) as b:
                for k in range(QT):
                    row = bass.ds(QT * b + ORDER[k], 1)
                    sp.wait_ge(fin_done, QT * b + k + 1 + SLOTS)
                    sp.dma_start(out_v[:, row, :], x_sb[:, row, :]).then_inc(out_done, 16)
            sp.wait_ge(out_done, 16 * NT)

        @block.gpsimd
        def _(pool):
            seq = Sequence(pool, pool_seq)
            pool.sem_inc(fadd_done, SLOTS)
            nc.gpsimd.memset(table_in[:], 0.0).then_inc(table_ready, 1)
            seq.mark(nc.gpsimd.memset(neg_half[:], -0.5))
            seq.mark(nc.gpsimd.memset(ident[:], 0.0))
            seq.settle()
            nc.gpsimd.affine_select(out=ident[:], in_=ident[:], compare_op=ALU.not_equal, fill=1.0,
                                    base=0, pattern=[[-1, P]], channel_multiplier=1).then_inc(consts, 1)
            nc.gpsimd.memset(xn_ring[:, :, :, C:C + 1], 1.0).then_inc(consts, 1)
            nc.gpsimd.memset(ones[:], 1.0).then_inc(consts, 1)
            seq.mark(nc.gpsimd.memset(ident_bf[:], 0.0))
            seq.mark(nc.gpsimd.memset(mask_bf[:], 0.0))
            seq.mark(nc.gpsimd.memset(az[:], 0.0))

            def ln_norm(k):
                first, end = LN_BLOCKS[k]
                block_tiles = slice(first, end)
                pool.wait_ge(ln_arg_done, k + 1)
                seq.link(nc.gpsimd.tensor_tensor(ln_r[:, block_tiles], ln_arg[:, block_tiles], neg_half[:, 0:end - first], ALU.pow))
                pool.wait_ge(ln_nmean_done, k + 1)
                nc.gpsimd.tensor_tensor(ln_nb[:, block_tiles], ln_nmean[:, block_tiles], ln_r[:, block_tiles],
                                        ALU.mult).then_inc(ln_nb_done, 1)
                pool.wait_ge(ln_nb_done, k + 1)
                for g in range(first // GT, end // GT):
                    wait(pool, gram_done, g + 1 - XN_SLOTS)
                    for t in range(ACT_TILES[g], GT):
                        n = GT * g + t
                        nc.gpsimd.tensor_scalar(xn_ring[:, g % XN_SLOTS, t, 0:C], x_sb[:, n, :], ln_r[:, n:n + 1],
                                                ln_nb[:, n:n + 1], ALU.mult, ALU.add).then_inc(xn_pool, 1)

            ln_norm(0)
            ln_norm(1)
            ln_norm(2)
            ln_norm(3)
            seq.settle()
            pool.wait_ge(lora_in, 16)
            for m in range(3):
                spread = az[:, m, :].rearrange("r (i three) -> r i three", three=3)[:, :, m]
                nc.gpsimd.tensor_copy(spread, lora_sb[:, L_AT:L_AT + C]).then_inc(consts, 1)
            ln_norm(4)
            ln_norm(5)
            pool.wait_ge(lnw_red, 1)
            nc.gpsimd.partition_all_reduce(lnw_abs[:, 1:2], lnw_abs[:, 0:1], P, REDUCE_ABSMAX).then_inc(lnw_all, 1)

            def normalise(g, u):
                pool.wait_ge(farg_done, 3 * (g + 1))
                seq.link(nc.gpsimd.tensor_tensor(f_r[:, u, 0, :], f_arg[:, u, 0, :], neg_half[:, 0:GT], ALU.pow))
                nc.gpsimd.tensor_tensor(f_r[:, u, 1, :], f_r[:, u, 0, :], f_arg[:, u, 1, :], ALU.mult).then_inc(fr_done, 1)
                pool.wait_ge(fr_done, g + 1)
                if g == NG - 1:
                    pool.wait_ge(m_abs, 2)
                    nc.gpsimd.partition_all_reduce(amax[:, 2:4], amax[:, 0:2], P, REDUCE_ABSMAX).then_inc(m_all, 1)
                for t in range(GT - 1):
                    nc.gpsimd.tensor_scalar(g_ring[:, u, t, :], g_ring[:, u, t, :], f_r[:, u, 0, t:t + 1],
                                            f_r[:, u, 1, t:t + 1], ALU.mult, ALU.add).then_inc(z_pool, 1)

            def f_add(g):
                pool.wait_ge(fout_done, g + 1)
                rows = x_sb[:, GT * g:GT * (g + 1), :].rearrange("p t c -> p (t c)")
                nc.gpsimd.tensor_tensor(rows, rows, f_out[:, g % 2, :], ALU.add).then_inc(fadd_done, 1)

            for g in range(NG):
                normalise(g, g % 2)
                if g == 0:
                    nc.gpsimd.tensor_copy(lnb_bc[:], lnb_c.unsqueeze(2).broadcast_to([P, HC, P])).then_inc(lnb_done, 1)
                if g == 1:
                    pool.wait_ge(wq_pf_done, 1)
                    nc.gpsimd.tensor_copy(wq_pf32[:], wq_pf[:]).then_inc(pf32_done, 1)
                if g == 2:
                    pool.wait_ge(bn_sums, 4)
                    seq.link(nc.gpsimd.tensor_tensor(bn[:, 2, :], bn[:, 1, :], bn[:, 1, :], ALU.mult))
                    seq.link(nc.gpsimd.tensor_tensor(bn[:, 3, :], bn[:, 0, :], bn[:, 2, :], ALU.subtract))
                    seq.link(nc.gpsimd.tensor_scalar(bn[:, 4, :], bn[:, 3, :], 0.0, BN_EPS, ALU.max, ALU.add))
                    seq.mark(nc.gpsimd.tensor_tensor(bn[:, 5, :], bn[:, 4, :], neg_half[:, 0:3], ALU.pow))
                if g == 3:
                    seq.link(nc.gpsimd.tensor_tensor(bn[:, 6, :], gamma_c, bn[:, 5, :], ALU.mult))
                    seq.link(nc.gpsimd.tensor_tensor(bn[:, 7, :], bn[:, 1, :], bn[:, 6, :], ALU.mult))
                    seq.link(nc.gpsimd.tensor_tensor(bn[:, 8, :], beta_c, bn[:, 7, :], ALU.subtract))
                    seq.mark(nc.gpsimd.tensor_tensor(bn[:, 9, 0:1], bn[:, 6, 0:1], bn[:, 6, 1:2], ALU.mult))
                    nc.gpsimd.tensor_tensor(bn[:, 10, 0:1], bn[:, 8, 0:1], bn[:, 6, 1:2], ALU.mult).then_inc(bn_w, 1)
                if g == 4:
                    seq.settle()
                    nc.gpsimd.tensor_scalar(wq_scaled[:], wm[:, 0, :], bn[:, 9, 0:1], None, ALU.mult).then_inc(bn_w, 1)
                if g == 5:
                    nc.gpsimd.tensor_scalar(wv_scaled[:], wm[:, 2, :], bn[:, 6, 2:3], None, ALU.mult).then_inc(bn_w, 1)
                    nc.gpsimd.tensor_copy(bv_bc[:], bn[:, 8, 2:3].broadcast_to([P, P])).then_inc(bn_w, 1)
                if g >= 3:
                    f_add(g - 3)
            f_add(NG - 3)
            nc.gpsimd.affine_select(out=ident_bf[:], in_=ident_bf[:], compare_op=ALU.not_equal, fill=1.0,
                                    base=0, pattern=[[-1, P]], channel_multiplier=1).then_inc(consts, 1)
            nc.gpsimd.affine_select(out=mask_bf[:], in_=mask_bf[:], compare_op=ALU.is_ge, fill=MASKED,
                                    base=0, pattern=[[-1, P]], channel_multiplier=1).then_inc(consts, 1)

            def bias_add(g, after_ffn=True):
                if after_ffn:
                    pool.wait_ge(fadd_done, g + 1 + SLOTS)
                pool.wait_ge(bias_done, GT + 2)
                nc.gpsimd.tensor_tensor(x_sb[:, bass.ds(GT * g, GT), :], x_sb[:, bass.ds(GT * g, GT), :], bias4[:],
                                        ALU.add).then_inc(badd_done, 1)

            with pool.Fori(0, NG - 2) as g:
                bias_add(g)
            f_add(NG - 2)
            bias_add(NG - 2)
            bias_add(NG - 1, after_ffn=False)

            def exp_bias(b, k):
                n, par = QT * b + k, k % 2
                pool.wait_ge(max_done, n + 1)
                nc.gpsimd.tensor_tensor(nbias[:, par:par + 1], nmax[:, par:par + 1], amax[:, 8:9],
                                        ALU.mult).then_inc(nb_done, 1)

            def scale_sum(b, k):
                n, slot = QT * b + k, k % 4
                pool.wait_ge(exp_done, n + 1 + SLOTS)
                nc.gpsimd.tensor_tensor(rowsum_s[:, slot:slot + 1], rowsum[:, slot:slot + 1], amax[:, 10:11],
                                        ALU.mult).then_inc(sum_done, 1)

            exp_bias(0, 0)
            exp_bias(0, 1)
            pool.wait_ge(badd_done, NG)
            f_add(NG - 1)

            def attend(b, last):
                for k in range(QT):
                    scale_sum(b, k)
                    if k + 2 < QT:
                        exp_bias(b, k + 2)
                    elif not last:
                        exp_bias(b + 1, k + 2 - QT)

            with pool.Fori(0, BATCH - 1) as b:
                attend(b, False)
            attend(BATCH - 1, True)

        @block.scalar
        def _(act):
            act.dma_start(lora_sb[:], lora_d[:, :]).then_inc(lora_in, 16)
            act.sem_inc(exp_done, SLOTS)

            act.wait_ge(table_ready, 1)
            nc.scalar.activation(table_out[:, 0:1], table_in[:], ACT.Gelu).then_inc(table_ready, 1)

            def weight_sum(k, col, arrived):
                act.wait_ge(arrived, 16)
                wait(act, wabs_done, k)
                nc.scalar.activation(abs_junk[:], w_sb[:, col:col + H], ACT.Abs, accum_out=wabs[:, k:k + 1]).then_inc(wabs_done, 1)

            def ln_norm(g):
                act.wait_ge(ln_nb_done, LN_BLOCK_OF[g] + 1)
                wait(act, gram_done, g + 1 - XN_SLOTS)
                for t in range(ACT_TILES[g]):
                    n = GT * g + t
                    nc.scalar.activation(xn_ring[:, g % XN_SLOTS, t, 0:C], x_sb[:, n, :], ACT.Identity,
                                         bias=ln_nb[:, n:n + 1], scale=ln_r[:, n:n + 1]).then_inc(xn_act, 1)

            def x_hi(g):
                act.wait_ge(xT_done, g + 1)
                nc.scalar.activation(xT_hi[:, tokens(GT * g, GT)], banks[:, XT_BANKS[g % 2], :], ACT.Copy).then_inc(xhi_done, 1)

            def gelu(g, u, t):
                act.wait_ge(h_done, GT * g + t + 1)
                if t == 0:
                    wait(act, zT_done, HC * (g - 1))
                nc.scalar.activation(g_ring[:, u, t, :], banks[:, t % 2, :], ACT.Gelu, scale=1.0 / XS).then_inc(gelu_done, 1)

            ln_norm(0)
            ln_norm(1)
            x_hi(0)
            ln_norm(2)
            x_hi(1)
            weight_sum(0, W_FC, wfc_in)
            ln_norm(3)
            x_hi(2)
            ln_norm(4)
            x_hi(3)
            weight_sum(1, W_PF, w_in)
            ln_norm(5)
            x_hi(4)
            gelu(0, 0, 0)
            gelu(0, 0, 1)
            ln_norm(6)
            gelu(0, 0, 2)
            gelu(0, 0, 3)
            x_hi(5)
            ln_norm(7)
            x_hi(6)
            gelu(1, 1, 0)
            gelu(1, 1, 1)
            x_hi(7)
            act.wait_ge(gram_done, NG)
            nc.scalar.activation(gram[:], banks[:, 7, 0:C + 1], ACT.Copy).then_inc(gram_cp, 1)

            def z_high(g, u):
                for c in range(HC):
                    act.wait_ge(zT_done, HC * g + c + 1)
                    if c == 0:
                        wait(act, f_done, g - 1)
                        act.wait_ge(lnw_done, 1)
                    nc.scalar.activation(z_hi[:, u, c, :], banks[:, ZT_BANKS[c], :], ACT.Copy,
                                         scale=lnw_s[:, c:c + 1]).then_inc(zhi_done, 1)

            def z_norm(g, u):
                act.wait_ge(fr_done, g + 1)
                nc.scalar.activation(g_ring[:, u, 3, :], g_ring[:, u, 3, :], ACT.Identity, bias=f_r[:, u, 1, 3:4],
                                     scale=f_r[:, u, 0, 3:4]).then_inc(z_act, 1)

            def f_scaled(g, u):
                act.wait_ge(f_done, g + 1)
                act.wait_ge(fadd_done, g - 1 + SLOTS)
                nc.scalar.activation(f_out[:, u, :], banks[:, 4, :], ACT.Copy, scale=ffn_scale[:, 0:1]).then_inc(fout_done, 1)

            def ffn_step(g, u, between=None):
                gelu(g, u, 0)
                gelu(g, u, 1)
                if not isinstance(g, int) or g >= 3:
                    f_scaled(g - 3, 1 - u)
                z_norm(g - 1, 1 - u)
                gelu(g, u, 2)
                gelu(g, u, 3)
                if between:
                    between()
                if isinstance(g, int) and g == NG - 1:
                    nc.scalar.activation(table_out[:, 1:2], table_in[:], ACT.Exp).then_inc(table_ready, 1)
                z_high(g - 1, 1 - u)

            gelu(1, 1, 2)
            gelu(1, 1, 3)
            z_norm(0, 0)
            act.wait_ge(prep_mm, 2)
            nc.scalar.activation(wmT[:], banks[:, 4, 0:3 * C], ACT.Copy).then_inc(prep_wm, 1)
            nc.scalar.activation(woT[:], banks[:, 4, 3 * C:4 * C], ACT.Copy).then_inc(woT_done, 1)
            z_high(0, 0)

            def combined_weights():
                act.wait_ge(prep_mm, 3)
                act.wait_ge(two_mm, 1)
                nc.scalar.activation(wm[:].rearrange("p j c -> p (j c)"), banks[:, 7, 0:3 * C], ACT.Copy).then_inc(prep_wm, 1)
                nc.scalar.activation(two_proj[:], banks[:, 7, 3 * C:4 * C], ACT.Copy).then_inc(two_done, 1)

            ffn_step(2, 0, between=combined_weights)
            with act.Fori(1, 3) as p:
                ffn_step(2 * p + 1, 1)
                ffn_step(2 * p + 2, 0)
            ffn_step(7, 1)
            z_norm(7, 1)
            f_scaled(5, 1)
            act.wait_ge(m_scale, 1)
            nc.scalar.activation(m_hi[:], banks[:, 7, 0:C], ACT.Copy, scale=amax[:, 6:7]).then_inc(bias_done, 1)
            nc.scalar.activation(u_hi_w[:], banks[:, 7, C + 1:2 * C + 1], ACT.Copy, scale=amax[:, 7:8]).then_inc(bias_done, 1)
            for t in range(GT):
                nc.scalar.activation(bias4[:, t, :], banks[:, 7, 257:257 + C], ACT.Copy).then_inc(bias_done, 1)

            def q_high(g, slot):
                act.wait_ge(q_mm, g + 1)
                nc.scalar.activation(qT_hi[:, tokens(GT * g, GT)], banks[:, Q_BANKS[slot], :], ACT.Identity,
                                     bias=amax[:, 9:10]).then_inc(qhi_done, 1)

            def u_high(g, slot):
                act.wait_ge(u_mm, g + 1)
                nc.scalar.activation(u_hi[:, bass.ds(GT * g, GT), :], banks[:, U_BANKS[slot], :], ACT.Copy).then_inc(uhi_done, 1)

            z_high(7, 1)
            act.wait_ge(m_split, 3)
            q_high(0, 1)
            u_high(0, 1)
            f_scaled(6, 0)
            q_high(1, 2)
            u_high(1, 2)
            with act.Fori(0, 2) as p:
                for slot in range(QU_SLOTS):
                    q_high(QU_SLOTS * p + 2 + slot, slot)
                    u_high(QU_SLOTS * p + 2 + slot, slot)

            def exps(b, k):
                n, par, slot, width = QT * b + k, k % 2, k % 4, P * (ORDER[k] + 1)
                act.wait_ge(nb_done, n + 1)
                transposed = CHUNK0[k - 1] if k else -CHUNKS[QT - 1]
                wait(act, eT_done, BATCH_CHUNKS * b + transposed + SLOTS)
                nc.scalar.activation(e_ring[:, par, 0:width],
                                     banks[:, 2 * par:2 * par + 2, :].rearrange("p a n -> p (a n)")[:, 0:width],
                                     ACT.Exp, bias=nbias[:, par:par + 1], scale=amax[:, 8:9],
                                     accum_out=rowsum[:, slot:slot + 1]).then_inc(exp_done, 1)

            def e_high(b, k):
                n, par, blocks = QT * b + k, k % 2, ORDER[k] + 1
                act.wait_ge(pv_done, n - 1 + SLOTS)
                for c in range(CHUNKS[k]):
                    j0, j1 = GT * c, min(GT * (c + 1), blocks)
                    act.wait_ge(eT_done, BATCH_CHUNKS * b + CHUNK0[k] + c + 1 + SLOTS)
                    nc.scalar.activation(eT_hi[:, par, j0:j1, :], banks[:, 5 + (CHUNK0[k] + c) % 2, 0:P * (j1 - j0)],
                                         ACT.Copy, scale=ES).then_inc(ehi_done, 1)

            exps(0, 0)
            f_scaled(7, 1)
            e_high(0, 0)
            exps(0, 1)

            def attend(b, last):
                for k in range(QT):
                    if k + 1 < QT:
                        e_high(b, k + 1)
                    elif not last:
                        e_high(b + 1, 0)
                    if k + 2 < QT:
                        exps(b, k + 2)
                    elif not last:
                        exps(b + 1, k + 2 - QT)

            with act.Fori(0, BATCH - 1) as b:
                attend(b, False)
            attend(BATCH - 1, True)

        @block.vector
        def _(dve):
            seq = Sequence(dve, dve_seq)
            dve.sem_inc(qlo_done, SLOTS)
            dve.sem_inc(ulo_done, SLOTS)
            dve.sem_inc(fin_done, SLOTS)
            dve.sem_inc(elo_done, SLOTS)

            def x_low(g):
                dve.wait_ge(xhi_done, g + 1)
                nc.vector.tensor_tensor(xT_lo[:, tokens(GT * g, GT)], banks[:, XT_BANKS[g % 2], :],
                                        xT_hi[:, tokens(GT * g, GT)], ALU.subtract).then_inc(xlo_done, 1)

            def threshold(k):
                dve.wait_ge(thr_sum, k + 1)
                for part, sign in enumerate((1.0, -1.0)):
                    seq.mark(nc.vector.tensor_scalar(thr[:, 2 * k + part:2 * k + part + 1], banks[:, 4, 0:1],
                                                     sign * 0.5 / (H * C), sign * 0.5 * Q_EPS, ALU.mult, ALU.add))
                seq.settle()

            def quantise(k, src, dst):
                seq.link(nc.vector.tensor_scalar(below[:], src, thr[:, 2 * k + 1:2 * k + 2], None, ALU.is_lt))
                return nc.vector.scalar_tensor_tensor(dst, src, thr[:, 2 * k:2 * k + 1], below[:], ALU.is_gt, ALU.subtract)

            def ln_block(k, between=()):
                first, end = LN_BLOCKS[k]
                dve.wait_ge(x_in[k], 16)
                for n in range(first, end + 1):
                    if n < end:
                        seq.mark(nc.vector.bn_stats(ln_st[:, n, :], x_sb[:, n, :]))
                    if n > first:
                        seq.settle(1 if n < end else 0)
                        seq.mark(nc.vector.bn_aggr(ln_mv[:, n - 1, :], ln_st[:, n - 1, :]))
                for g in between:
                    x_low(g)
                seq.settle()
                nc.vector.tensor_scalar(ln_arg[:, first:end], ln_mv[:, first:end, 1], 1.0 / (XS * XS), LN_EPS / (XS * XS),
                                        ALU.mult, ALU.add).then_inc(ln_arg_done, 1)
                nc.vector.tensor_scalar(ln_nmean[:, first:end], ln_mv[:, first:end, 0], -1.0, None,
                                        ALU.mult).then_inc(ln_nmean_done, 1)

            def f_stats(g, u, between=None):
                def aggregate(t):
                    seq.mark(nc.vector.bn_aggr(f_mv[:, u, t, :], fst[:, u, t, :]))

                def negate(at):
                    nc.vector.tensor_scalar(f_arg[:, u, 1, at], f_mv[:, u, at, 0], -1.0, None, ALU.mult).then_inc(farg_done, 1)

                for t in range(GT):
                    if t == 2 and between:
                        between()
                    dve.wait_ge(gelu_done, GT * g + t + 1)
                    if t == GT - 1:
                        seq.settle(1)
                    seq.mark(nc.vector.bn_stats(fst[:, u, t, :], g_ring[:, u, t, :]))
                aggregate(0)
                aggregate(1)
                seq.settle(1)
                negate(slice(0, 1))
                aggregate(2)
                aggregate(3)
                seq.settle()
                nc.vector.tensor_scalar(f_arg[:, u, 0, :], f_mv[:, u, :, 1], LN_EPS, None, ALU.add).then_inc(farg_done, 1)
                negate(slice(1, GT))

            F_STATS = 2 * GT

            ln_block(0)
            ln_block(1)
            ln_block(2)
            ln_block(3)
            x_low(0)
            ln_block(4, (1,))
            threshold(0)
            quantise(0, w_sb[:, W_FC:W_FC + H], wq_fc[:]).then_inc(wq_fc_done, 1)
            x_low(2)
            ln_block(5, (3,))
            threshold(1)
            quantise(1, w_sb[:, W_PF:W_PF + H], wq_pf[:].rearrange("p k c -> p (k c)")).then_inc(wq_pf_done, 1)
            x_low(4)
            nc.vector.tensor_reduce(lnw_abs[:, 0:1], lnw_c, axis=AXX, op=ALU.max,
                                    apply_absolute_value=True).then_inc(lnw_red, 1)
            f_stats(0, 0)
            x_low(5)
            x_low(6)
            dve.wait_ge(lnw_all, 1)
            seq.link(nc.vector.tensor_scalar(ffn_scale[:, 0:1], lnw_abs[:, 1:2], 1.0 / ZS, 1e-30, ALU.mult, ALU.max))
            seq.link(nc.vector.reciprocal(ffn_scale[:, 1:2], ffn_scale[:, 0:1]))
            nc.vector.tensor_scalar(lnw_s[:], lnw_c, ffn_scale[:, 1:2], None, ALU.mult).then_inc(lnw_done, 1)

            def z_low(g, u, chunks=range(HC)):
                wait(dve, f_done, g - 1)
                for c in chunks:
                    dve.wait_ge(zhi_done, HC * g + c + 1)
                    nc.vector.scalar_tensor_tensor(z_lo[:, u, c, :], banks[:, ZT_BANKS[c], :], lnw_s[:, c:c + 1],
                                                   z_hi[:, u, c, :], ALU.mult, ALU.subtract).then_inc(zlo_done, 1)

            f_stats(1, 1, between=lambda: x_low(7))
            z_low(0, 0)
            f_stats(2, 0)
            dve.wait_ge(bn_z, 1)
            dve.wait_ge(prep_wm, 2)
            zb = banks[:, 4, 0:3 * (C + 1)].rearrange("p (j c) -> p j c", j=3)
            for j in range(3):
                nc.vector.tensor_tensor_reduce(out=bn_prod[:, j, :], in0=zb[:, j, 0:C], in1=wm[:, j, :],
                                               scale=1.0 / (XS * XS * TOKENS), scalar=0.0, op0=ALU.mult, op1=ALU.add,
                                               accum_out=bn[:, 0, j:j + 1]).then_inc(bn_sums, 1)
            nc.vector.tensor_scalar(bn[:, 1, :], zb[:, :, C], 1.0 / (XS * TOKENS), None, ALU.mult).then_inc(bn_sums, 1)
            z_low(1, 1)
            start = seq.count
            with dve.Fori(1, 3) as p:
                seq.count = start + 2 * F_STATS * (p - 1)
                f_stats(2 * p + 1, 1)
                z_low(2 * p, 0)
                f_stats(2 * p + 2, 0)
                z_low(2 * p + 1, 1)
            seq.count = start + 4 * F_STATS
            f_stats(7, 1)
            dve.wait_ge(m_mm, 1)
            m_ps, u_ps = banks[:, 7, 0:C + 1], banks[:, 7, C + 1:2 * C + 1]
            nc.vector.tensor_reduce(amax[:, 0:1], m_ps, axis=AXX, op=ALU.max, apply_absolute_value=True).then_inc(m_abs, 1)
            nc.vector.tensor_reduce(amax[:, 1:2], u_ps, axis=AXX, op=ALU.max, apply_absolute_value=True).then_inc(m_abs, 1)
            z_low(6, 0, (0, 1))
            dve.wait_ge(m_all, 1)
            seq.mark(nc.vector.tensor_scalar(amax[:, 4:5], amax[:, 2:3], 1.0, 1.0 / MS, ALU.max, ALU.mult))
            seq.mark(nc.vector.tensor_scalar(amax[:, 5:6], amax[:, 3:4], 1e-30, 1.0 / MS, ALU.max, ALU.mult))
            seq.link(nc.vector.tensor_scalar(m_bias[:], m_ps[:, C:C + 1], XS, None, ALU.mult))
            nc.vector.reciprocal(amax[:, 6:8], amax[:, 4:6]).then_inc(m_scale, 1)
            seq.mark(nc.vector.tensor_scalar(amax[:, 8:9], amax[:, 4:5], float(C) ** -0.5 / (XS * XS), None, ALU.mult))
            z_low(6, 0, (2, 3))
            dve.wait_ge(m_scale, 1)
            nc.vector.tensor_tensor(amax[:, 9:10], m_bias[:], amax[:, 6:7], ALU.mult).then_inc(m_split, 1)
            seq.mark(nc.vector.tensor_scalar(amax[:, 10:11], amax[:, 7:8], XS * ES, None, ALU.mult))
            dve.wait_ge(bias_done, GT + 2)
            nc.vector.scalar_tensor_tensor(m_lo[:], m_ps[:, 0:C], amax[:, 6:7], m_hi[:], ALU.mult, ALU.subtract)\
                .then_inc(m_split, 1)
            nc.vector.scalar_tensor_tensor(u_lo_w[:], u_ps, amax[:, 7:8], u_hi_w[:], ALU.mult, ALU.subtract)\
                .then_inc(m_split, 1)
            seq.settle()

            def q_low(g, slot):
                dve.wait_ge(qhi_done, g + 1)
                nc.vector.scalar_tensor_tensor(qT_lo[:, tokens(GT * g, GT)], banks[:, Q_BANKS[slot], :], amax[:, 9:10],
                                               qT_hi[:, tokens(GT * g, GT)], ALU.add, ALU.subtract).then_inc(qlo_done, 1)

            def u_low(g, slot):
                dve.wait_ge(uhi_done, g + 1)
                nc.vector.tensor_tensor(u_lo[:, bass.ds(GT * g, GT), :],
                                        banks[:, U_BANKS[slot], :].rearrange("p (t c) -> p t c", t=GT),
                                        u_hi[:, bass.ds(GT * g, GT), :], ALU.subtract).then_inc(ulo_done, 1)

            z_low(7, 1)
            for g in range(2):
                q_low(g, g + 1)
                u_low(g, g + 1)
            with dve.Fori(0, 2) as p:
                for slot in range(QU_SLOTS):
                    q_low(QU_SLOTS * p + 2 + slot, slot)
                    u_low(QU_SLOTS * p + 2 + slot, slot)

            def row_max(b, k):
                n, par = QT * b + k, k % 2
                dve.wait_ge(s_done, n + 1)
                nc.vector.tensor_reduce(
                    nmax[:, par:par + 1],
                    banks[:, 2 * par:2 * par + 2, :].rearrange("p a n -> p (a n)")[:, 0:P * (ORDER[k] + 1)],
                    axis=AXX, op=ALU.max, negate=True).then_inc(max_done, 1)

            def e_low(b, k):
                n, par = QT * b + k, k % 2
                dve.wait_ge(pv_done, n - 1 + SLOTS)
                for c in range(CHUNKS[k]):
                    j0, j1 = GT * c, min(GT * (c + 1), ORDER[k] + 1)
                    dve.wait_ge(ehi_done, BATCH_CHUNKS * b + CHUNK0[k] + c + 1)
                    nc.vector.scalar_tensor_tensor(eT_lo[:, par, j0:j1, :].rearrange("p j t -> p (j t)"),
                                                   banks[:, 5 + (CHUNK0[k] + c) % 2, 0:P * (j1 - j0)], ES,
                                                   eT_hi[:, par, j0:j1, :].rearrange("p j t -> p (j t)"),
                                                   ALU.mult, ALU.subtract).then_inc(elo_done, 1)

            def row_inverse(b, k):
                n, slot = QT * b + k, k % 4
                dve.wait_ge(sum_done, n + 1)
                seq.mark(nc.vector.reciprocal(rinv[:, slot:slot + 1], rowsum_s[:, slot:slot + 1]))

            def finish(b, k):
                n, slot = QT * b + k, k % 4
                seq.settle()
                dve.wait_ge(pv_done, n + 1 + SLOTS)
                dve.wait_ge(badd_done, 2 * (b + 1))
                row = x_sb[:, bass.ds(QT * b + ORDER[k], 1), :].rearrange("p o c -> p (o c)")
                nc.vector.scalar_tensor_tensor(row, banks[:, 4 + 3 * (k % 2), 0:C], rinv[:, slot:slot + 1], row,
                                               ALU.mult, ALU.add).then_inc(fin_done, 1)

            row_max(0, 0)
            row_max(0, 1)
            e_low(0, 0)

            def attend(b, last):
                for k in range(QT):
                    if k + 2 < QT:
                        row_max(b, k + 2)
                    elif not last:
                        row_max(b + 1, k + 2 - QT)
                    row_inverse(b, k)
                    if k + 1 < QT:
                        e_low(b, k + 1)
                    elif not last:
                        e_low(b + 1, 0)
                    finish(b, k)

            start = seq.count
            with dve.Fori(0, BATCH - 1) as b:
                seq.count = start + QT * b
                attend(b, False)
            seq.count = start + QT * (BATCH - 1)
            dve.wait_ge(fadd_done, NG + SLOTS)
            attend(BATCH - 1, True)

        @block.tensor
        def _(pe):
            mm = nc.tensor.matmul
            pe.sem_inc(eT_done, SLOTS)
            pe.sem_inc(pv_done, SLOTS)

            def ln_products(g):
                slot = g % XN_SLOTS
                pe.wait_ge(xn_act, sum(ACT_TILES[:g + 1]))
                pe.wait_ge(xn_pool, GT * (g + 1) - sum(ACT_TILES[:g + 1]))
                wait(pe, xlo_done, g - 1)
                for t in range(GT):
                    last = nc.tensor.transpose(banks[:, XT_BANKS[g % 2], tokens(t)], xn_ring[:, slot, t, 0:C], ident[:])
                last.then_inc(xT_done, 1)
                for t in range(GT):
                    last = mm(banks[:, 7, 0:C + 1], xn_ring[:, slot, t, 0:C], xn_ring[:, slot, t, :],
                              start=(g == 0 and t == 0), stop=(g == NG - 1 and t == GT - 1))
                last.then_inc(gram_done, 1)

            def ffn_up(g, tiles):
                for t in tiles:
                    n = GT * g + t
                    wait(pe, gelu_done, n - 1)
                    if t in (0, 2):
                        pe.wait_ge(xlo_done, g + 1)
                    mm(banks[:, t % 2, :], xT_hi[:, tokens(n)], wq_fc[:], start=True, stop=False)
                    mm(banks[:, t % 2, :], xT_lo[:, tokens(n)], wq_fc[:], start=False, stop=True).then_inc(h_done, 1)

            pe.wait_ge(consts, 1)
            for _ in range(WARM_UP):
                mm(banks[:, 0, 0:P], ident[:], ident[:], start=True, stop=True)
            pe.wait_ge(consts, 3)
            ln_products(0)
            ln_products(1)
            ln_products(2)
            pe.wait_ge(wabs_done, 1)
            mm(banks[:, 4, 0:1], ones[:], wabs[:, 0:1], start=True, stop=True).then_inc(thr_sum, 1)
            ln_products(3)
            ln_products(4)
            pe.wait_ge(wabs_done, 2)
            pe.wait_ge(wq_fc_done, 1)
            mm(banks[:, 4, 0:1], ones[:], wabs[:, 1:2], start=True, stop=True).then_inc(thr_sum, 1)
            ffn_up(0, (0, 1))
            ln_products(5)
            ffn_up(0, (2, 3))
            pe.wait_ge(w_in, 16)
            pe.wait_ge(lora_in, 16)
            pe.wait_ge(consts, 6)
            pe.wait_ge(wq_pf_done, 1)

            def lora_product(m):
                mm(banks[:, 4, 0:3 * C], lora_sb[:, L_B + C * m:L_B + C * (m + 1)], az[:, m, :], start=(m == 0), stop=False)

            lora_product(0)
            ln_products(6)
            ffn_up(1, (0, 1))
            lora_product(1)
            ln_products(7)
            ffn_up(1, (2, 3))
            lora_product(2)
            mm(banks[:, 4, 0:3 * C], ident[:], w_sb[:, W_QKVT:W_QKVT + 3 * C], start=False, stop=True).then_inc(prep_mm, 1)
            mm(banks[:, 4, 3 * C:4 * C], lora_sb[:, L_PB:L_PB + C], lora_sb[:, L_PAT:L_PAT + C], start=True, stop=False)
            mm(banks[:, 4, 3 * C:4 * C], ident[:], w_sb[:, W_OT:W_OT + C], start=False, stop=True).then_inc(prep_mm, 1)

            def z_transposes(g, u):
                pe.wait_ge(z_pool, 3 * (g + 1))
                pe.wait_ge(z_act, g + 1)
                for c in range(HC):
                    wait(pe, zlo_done, HC * (g - 1) + c + 1)
                    for t in range(GT):
                        last = nc.tensor.transpose(banks[:, ZT_BANKS[c], tokens(t)], g_ring[:, u, t, tokens(c)], ident[:])
                    last.then_inc(zT_done, 1)

            def ffn_down(g, u, tiles=range(GT)):
                for t in tiles:
                    if t == 0:
                        pe.wait_ge(zlo_done, HC * (g + 1))
                        wait(pe, fout_done, g)
                    for c in range(HC):
                        mm(banks[:, 4, tokens(t)], z_hi[:, u, c, tokens(t)], wq_pf[:, c, :], start=(c == 0), stop=False)
                        last = mm(banks[:, 4, tokens(t)], z_lo[:, u, c, tokens(t)], wq_pf[:, c, :],
                                  start=False, stop=(c == HC - 1))
                    if t == GT - 1:
                        last.then_inc(f_done, 1)

            def ffn_step(g, u):
                ffn_up(g, (2, 3))
                ffn_down(g - 2, u, (0, 1))
                z_transposes(g - 1, 1 - u)
                ffn_up(g + 1, (0, 1))
                ffn_down(g - 2, u, (2, 3))

            pe.wait_ge(xlo_done, NG)
            z_transposes(0, 0)
            ffn_up(2, (0, 1))
            pe.wait_ge(prep_wm, 1)
            pe.wait_ge(gram_cp, 1)
            for j in range(3):
                last = nc.tensor.transpose(banks[:, 7, tokens(j)], wmT[:, tokens(j)], ident[:])
            last.then_inc(prep_mm, 1)
            pe.wait_ge(woT_done, 1)
            mm(banks[:, 7, 3 * C:4 * C], w_sb[:, W_O:W_O + C], woT[:], start=True, stop=True).then_inc(two_mm, 1)
            for j in range(3):
                last = mm(banks[:, 4, (C + 1) * j:(C + 1) * (j + 1)], wmT[:, C * j:C * (j + 1)], gram[:], start=True, stop=True)
            last.then_inc(bn_z, 1)
            ffn_up(2, (2, 3))
            z_transposes(1, 1)
            ffn_up(3, (0, 1))
            pe.wait_ge(bn_sums, 4)
            ffn_down(0, 0)
            with pe.Fori(1, 3) as p:
                ffn_step(2 * p + 1, 1)
                ffn_step(2 * p + 2, 0)
            ffn_up(7, (2, 3))
            ffn_down(5, 1, (0, 1))
            pe.wait_ge(bn_w, 4)
            pe.wait_ge(two_done, 1)
            pe.wait_ge(pf32_done, 1)
            pe.wait_ge(lnb_done, 1)
            mm(banks[:, 7, 0:C], wq_scaled[:], wm[:, 1, :], start=True, stop=True)
            mm(banks[:, 7, C:C + 1], wm[:, 1, :], bn[:, 10, 0:1], start=True, stop=True)
            mm(banks[:, 7, C + 1:2 * C + 1], wv_scaled[:], two_proj[:], start=True, stop=True)
            mm(banks[:, 7, 257:257 + C], bv_bc[:], two_proj[:], start=True, stop=False)
            for c in range(HC):
                last = mm(banks[:, 7, 257:257 + C], lnb_bc[:, c, :], wq_pf32[:, c, :], start=False, stop=(c == HC - 1))
            last.then_inc(m_mm, 1)
            z_transposes(6, 0)
            ffn_down(5, 1, (2, 3))

            def queries(g, slot):
                xs, to = tokens(GT * g, GT), banks[:, Q_BANKS[slot], :]
                wait(pe, qlo_done, g - 2 + SLOTS)
                mm(to, m_hi[:], xT_hi[:, xs], start=True, stop=False)
                mm(to, m_hi[:], xT_lo[:, xs], start=False, stop=False)
                mm(to, m_lo[:], xT_hi[:, xs], start=False, stop=True).then_inc(q_mm, 1)

            def values(g, slot):
                wait(pe, ulo_done, g - 2 + SLOTS)
                for t in range(GT):
                    n, to = GT * g + t, banks[:, U_BANKS[slot], tokens(t)]
                    mm(to, xT_hi[:, tokens(n)], u_hi_w[:], start=True, stop=False)
                    mm(to, xT_hi[:, tokens(n)], u_lo_w[:], start=False, stop=False)
                    last = mm(to, xT_lo[:, tokens(n)], u_hi_w[:], start=False, stop=True)
                last.then_inc(u_mm, 1)

            z_transposes(7, 1)
            pe.wait_ge(m_split, 3)
            pe.wait_ge(bias_done, GT + 2)
            queries(0, 1)
            values(0, 1)
            ffn_down(6, 0)
            queries(1, 2)
            pe.wait_ge(zlo_done, HC * NG)
            values(1, 2)
            with pe.Fori(0, 2) as p:
                for slot in range(QU_SLOTS):
                    queries(QU_SLOTS * p + 2 + slot, slot)
                    values(QU_SLOTS * p + 2 + slot, slot)

            def scores(b, k):
                n, par, width = QT * b + k, k % 2, P * (ORDER[k] + 1)
                pe.wait_ge(exp_done, n - 1 + SLOTS)
                for c in range(CHUNKS[k]):
                    lo, hi = 512 * c, min(512 * (c + 1), width)
                    to, keys = banks[:, 2 * par + c, 0:hi - lo], bass.ds(T * b + lo, hi - lo)
                    query = tokens(QT * b + ORDER[k])
                    diagonal = c == CHUNKS[k] - 1
                    mm(to, qT_hi[:, query], xT_hi[:, keys], start=True, stop=False)
                    mm(to, qT_hi[:, query], xT_lo[:, keys], start=False, stop=False)
                    last = mm(to, qT_lo[:, query], xT_hi[:, keys], start=False, stop=not diagonal)
                    if diagonal:
                        last = mm(banks[:, 2 * par + c, hi - lo - P:hi - lo], ident_bf[:], mask_bf[:], start=False, stop=True)
                last.then_inc(s_done, 1)

            def transpose_probs(b, k):
                n, par = QT * b + k, k % 2
                pe.wait_ge(exp_done, n + 1 + SLOTS)
                for c in range(CHUNKS[k]):
                    chunk = CHUNK0[k] + c
                    pe.wait_ge(elo_done, BATCH_CHUNKS * b + chunk - 1 + SLOTS)
                    for j in range(GT * c, min(GT * (c + 1), ORDER[k] + 1)):
                        last = nc.tensor.transpose(banks[:, 5 + chunk % 2, tokens(j - GT * c)], e_ring[:, par, tokens(j)],
                                                   ident[:])
                    last.then_inc(eT_done, 1)

            def attend_values(b, k):
                n, par, blocks = QT * b + k, k % 2, ORDER[k] + 1
                pe.wait_ge(elo_done, BATCH_CHUNKS * b + CHUNK0[k] + CHUNKS[k] + SLOTS)
                pe.wait_ge(fin_done, n - 1 + SLOTS)
                if k == 0:
                    pe.wait_ge(fout_done, NG)
                to = banks[:, 4 + 3 * par, 0:C]
                for j in range(blocks):
                    vh = u_hi[:, bass.ds(QT * b + j, 1), :].rearrange("p o c -> p (o c)")
                    vl = u_lo[:, bass.ds(QT * b + j, 1), :].rearrange("p o c -> p (o c)")
                    mm(to, eT_hi[:, par, j, :], vh, start=(j == 0), stop=False)
                    mm(to, eT_hi[:, par, j, :], vl, start=False, stop=False)
                    last = mm(to, eT_lo[:, par, j, :], vh, start=False, stop=(j == blocks - 1))
                last.then_inc(pv_done, 1)

            pe.wait_ge(consts, 8)
            pe.wait_ge(qlo_done, NG - 1 + SLOTS)
            scores(0, 0)
            ffn_down(7, 1)
            pe.wait_ge(qlo_done, NG + SLOTS)
            pe.wait_ge(ulo_done, NG + SLOTS)
            scores(0, 1)
            transpose_probs(0, 0)

            def attend(b, last):
                for k in range(QT):
                    if k + 2 < QT:
                        scores(b, k + 2)
                    elif not last:
                        scores(b + 1, k + 2 - QT)
                    if k + 1 < QT:
                        transpose_probs(b, k + 1)
                    elif not last:
                        transpose_probs(b + 1, 0)
                    attend_values(b, k)

            with pe.Fori(0, BATCH - 1) as b:
                attend(b, False)
            attend(BATCH - 1, True)


def kernel(L0_attn_x, L0_attn_W_attn, L0_attn_W_proj, L0_attn_lora_attn_A, L0_attn_lora_attn_B, L0_attn_lora_proj_A,
           L0_attn_lora_proj_B, L0_attn_bn_gamma, L0_attn_bn_beta, L0_ffn_W_fc, L0_ffn_ln_w, L0_ffn_ln_b, L0_ffn_W_proj):
    import numpy as np
    import concourse.bacc as bacc
    from concourse.bass_utils import run_bass_kernel_spmd

    def rows_to_partitions(a):
        return a.reshape(-1, P, a.shape[-1]).transpose(1, 0, 2).reshape(P, -1)

    a = {k: np.asarray(v) for k, v in dict(
        x=L0_attn_x, wa=L0_attn_W_attn, wo=L0_attn_W_proj, aA=L0_attn_lora_attn_A, aB=L0_attn_lora_attn_B,
        pA=L0_attn_lora_proj_A, pB=L0_attn_lora_proj_B, gamma=L0_attn_bn_gamma, beta=L0_attn_bn_beta, fc=L0_ffn_W_fc,
        lw=L0_ffn_ln_w, lb=L0_ffn_ln_b, pf=L0_ffn_W_proj).items()}
    weights = np.concatenate([
        a["fc"].T, rows_to_partitions(a["pf"].T), rows_to_partitions(a["wa"]), a["wa"].T, a["wo"], a["wo"].T,
        a["lw"].reshape(HC, P).T, a["lb"].reshape(HC, P).T, a["gamma"].reshape(3, P).T, a["beta"].reshape(3, P).T], axis=1)
    lora = np.concatenate([a["aA"].T, a["aB"], a["pA"].T, a["pB"]], axis=1)

    nc = bacc.Bacc("TRN2", target_bir_lowering=False, num_devices=1)
    arrays = {"x_dram": np.ascontiguousarray(a["x"]), "w_dram": np.ascontiguousarray(weights),
              "lora_dram": np.ascontiguousarray(lora)}
    ins = [nc.dram_tensor(n, v.shape, mybir.dt.from_np(v.dtype), kind="ExternalInput").ap() for n, v in arrays.items()]
    out = nc.dram_tensor("out_dram", a["x"].shape, F32, kind="ExternalOutput").ap()
    block_kernel(nc, *ins, out)
    r = run_bass_kernel_spmd(nc, [arrays], core_ids=[0])
    return r.results[0]["out_dram"]
```
